# Optimizing a Trainium2 kernel written in Bass

```python
import numpy as np
import jax
import jax.numpy as jnp

def _softmax(x, axis=-1):
    return jax.nn.softmax(x, axis=axis)

def _gelu(x):
    return jax.nn.gelu(x, approximate=True)

def _silu(x):
    return jax.nn.silu(x)

def _sigmoid(x):
    return jax.nn.sigmoid(x)

def _layernorm(x, axis=-1, eps=1e-05):
    m = jnp.mean(x, axis=axis, keepdims=True)
    v = jnp.var(x, axis=axis, keepdims=True)
    return (x - m) / jnp.sqrt(v + eps)

def _scatter_add(tgt, idx, src, axis=0):
    return tgt.at[idx].add(src)

def _segment_sum(src, seg, n):
    return jax.ops.segment_sum(src, seg, n)
kernel_name = 'mk_xattn_seq_d2_seqx_r2_1d3305'

def setup_inputs(seed: int=0):
    np.random.seed(seed)
    _w = jnp.asarray

    def _rec_inputs():
        import jax
        import jax.numpy as jnp
        _rk = jax.random.key(seed)
        x = -0.0003929 + 0.9999 * jax.random.normal(jax.random.fold_in(_rk, 1), (16, 512, 512), jnp.float32)
        _lenS = 512 - jax.random.randint(jax.random.fold_in(_rk, 7), (16,), 0, max(1, 512 // 4) + 1, jnp.int32)
        _lenS2 = 120 - jax.random.randint(jax.random.fold_in(_rk, 8), (16,), 0, max(1, 120 // 4) + 1, jnp.int32)
        _ctx_1024P = jax.random.normal(jax.random.fold_in(_rk, 11), (16, 16, 512), jnp.float32)
        _ctx_1024c = jax.random.dirichlet(jax.random.fold_in(_rk, 511), 0.3 * jnp.ones((16,), jnp.float32), (16, 120))
        _ctx_1024t = jnp.einsum('bsk,bkd->bsd', _ctx_1024c, _ctx_1024P)
        _ctx_1024t = _ctx_1024t * jax.lax.rsqrt(jnp.mean(jnp.square(_ctx_1024t)) + 1e-12) * 0.953939
        ctx_1024 = 2.81802e-05 + 1.00001 * (_ctx_1024t + 0.3 * jax.random.normal(jax.random.fold_in(_rk, 611), (16, 120, 512), jnp.float32))
        return (x, ctx_1024)
    x, ctx_1024 = _rec_inputs()

    def _L0_xattn_setup():
        import jax, jax.numpy as jnp
        import numpy as np
        B, L, D = (32, 256, 512)
        H, DK, DV = (8, 16, 16)

        def _xavier(key, shape):
            fan_in, fan_out = (shape[0], shape[1])
            std = (2.0 / (fan_in + fan_out)) ** 0.5
            return std * jax.random.normal(key, shape, dtype=jnp.float32)
        key = jax.random.key(seed)
        ks = jax.random.split(key, 11)
        return {'Q': jax.random.normal(ks[0], (B, L, D), jnp.float32), 'K': jax.random.normal(ks[1], (B, L, D), jnp.float32), 'V': jax.random.normal(ks[2], (B, L, D), jnp.float32), 'W_q': _xavier(ks[3], (D, H * DK)), 'W_k': _xavier(ks[4], (D, H * DK)), 'W_v': _xavier(ks[5], (D, H * DV)), 'W_o': _xavier(ks[6], (H * DV, D)), 'w1': _xavier(ks[7], (D, D)), 'b1': jnp.zeros((D,), jnp.float32), 'w2': _xavier(ks[8], (D, D)), 'b2': jnp.zeros((D,), jnp.float32)}
    _L0_xattn_all = _L0_xattn_setup()
    _L0_xattn_in = {k: v for k, v in _L0_xattn_all.items() if k in ('W_q', 'W_k', 'W_v', 'W_o', 'w1', 'b1', 'w2', 'b2')}
    del _L0_xattn_all

    def _L1_xattn_setup():
        import jax, jax.numpy as jnp
        import numpy as np
        B, SR, SF, D = (8, 1024, 1024, 512)
        key = jax.random.key(seed)
        k1, k2 = jax.random.split(key)
        H_real = jax.random.normal(k1, (B, SR, D), dtype=jnp.float32)
        H_fake = jax.random.normal(k2, (B, SF, D), dtype=jnp.float32)
        return {'H_real': H_real, 'H_fake': H_fake}
    _L1_xattn_all = _L1_xattn_setup()
    _L1_xattn_in = {k: v for k, v in _L1_xattn_all.items() if k in ()}
    del _L1_xattn_all
    return {'x': x, 'ctx_1024': ctx_1024, 'L0_xattn_W_q': _L0_xattn_in['W_q'], 'L0_xattn_W_k': _L0_xattn_in['W_k'], 'L0_xattn_W_v': _L0_xattn_in['W_v'], 'L0_xattn_W_o': _L0_xattn_in['W_o'], 'L0_xattn_w1': _L0_xattn_in['w1'], 'L0_xattn_b1': _L0_xattn_in['b1'], 'L0_xattn_w2': _L0_xattn_in['w2'], 'L0_xattn_b2': _L0_xattn_in['b2']}

def reference(x, ctx_1024, L0_xattn_W_q, L0_xattn_W_k, L0_xattn_W_v, L0_xattn_W_o, L0_xattn_w1, L0_xattn_b1, L0_xattn_w2, L0_xattn_b2):
    import jax
    import jax.numpy as jnp

    def _L0_xattn_ref(Q, K, V, W_q, W_k, W_v, W_o, w1, b1, w2, b2):
        import jax, jax.numpy as jnp
        import numpy as np
        B, L, D = (32, 256, 512)
        H, DK, DV = (8, 16, 16)

        def _xavier(key, shape):
            fan_in, fan_out = (shape[0], shape[1])
            std = (2.0 / (fan_in + fan_out)) ** 0.5
            return std * jax.random.normal(key, shape, dtype=jnp.float32)
        b, lq, _ = Q.shape
        lk = K.shape[1]
        Qh = (Q @ W_q).reshape(b, lq, H, DK)
        Kh = (K @ W_k).reshape(b, lk, H, DK)
        Vh = (V @ W_v).reshape(b, lk, H, DV)
        scale = 1.0 / jnp.sqrt(jnp.float32(DK))
        scores = jnp.einsum('bqhd,bkhd->bhqk', Qh, Kh) * scale
        attn = jax.nn.softmax(scores, axis=-1)
        ctx = jnp.einsum('bhqk,bkhd->bqhd', attn, Vh).reshape(b, lq, H * DV)
        attn_out = ctx @ W_o
        X = Q + attn_out
        h = jax.nn.relu(X @ w1.T + b1)
        ffn_out = h @ w2.T + b2
        return ffn_out + X

    def _L1_xattn_ref(H_real, H_fake):
        import jax, jax.numpy as jnp
        import numpy as np
        B, SR, SF, D = (8, 1024, 1024, 512)
        scores = jnp.einsum('brd,bfd->brf', H_real, H_fake)
        weights = jax.nn.softmax(scores, axis=-1)
        context = jnp.einsum('brf,bfd->brd', weights, H_fake)
        return H_real + context
    x = _L0_xattn_ref(x, ctx_1024, ctx_1024, L0_xattn_W_q, L0_xattn_W_k, L0_xattn_W_v, L0_xattn_W_o, L0_xattn_w1, L0_xattn_b1, L0_xattn_w2, L0_xattn_b2)
    x = _L1_xattn_ref(x, ctx_1024)
    return x

_drawn_inputs = setup_inputs


def setup_inputs(seed=0):
    import zlib

    import numpy as np

    out = dict(_drawn_inputs(seed))
    spreads = {'L0_xattn_b1': (0.0, 0.1), 'L0_xattn_b2': (0.0, 0.1)}
    factors = {}
    for name, (base, spread) in spreads.items():
        noise = np.random.default_rng([zlib.crc32(name.encode()), seed]).standard_normal(out[name].shape)
        drawn = base * np.exp(spread * noise) if base else spread * noise
        out[name] = jnp.asarray(drawn.astype(out[name].dtype))
    for name, factor in factors.items():
        out[name] = (out[name] * factor).astype(out[name].dtype)
    return out
```

```python
import concourse.bass as bass
from concourse import mybir
from concourse.alu_op_type import AluOpType
from contextlib import ExitStack

BATCHES, QUERIES, DIM, KEYS = 16, 512, 512, 120
HEADS, HEAD_DIM = 8, 16
PART = 128
CHUNKS = DIM // PART
TILES = QUERIES // PART
PROJ = HEADS * HEAD_DIM
HALF = HEADS // 2
SCALE = HEAD_DIM ** -0.5
LOW_HEADS = 6
LOW_ROWS = LOW_HEADS * HEAD_DIM
MAX_COLS = LOW_ROWS + HEADS
HEAD_ORDER = [0, 2, 4, 6, 1, 3, 5, 7]


def cross_attention_ffn_attention(nc, xT_d, ctx_d, ctxT_d, wq_d, wk_d, wv_d, wo_d, w1T_d, b1_d, w2T_d, b2_d,
                                  ident_d, head_rows_d, shift_rows_d, outT_d):
    fp32, fp32r = mybir.dt.float32, mybir.dt.float32r
    ACT, AX = mybir.ActivationFunctionType, mybir.AxisListType
    ADD, MULT = AluOpType.add, AluOpType.mult

    with ExitStack() as ctx:
        def sb(name, shape, dt=fp32):
            return ctx.enter_context(nc.sbuf_tensor(name, shape, dt))

        def bank(name):
            return ctx.enter_context(nc.psum_tensor(name, [PART, 512], fp32))

        def sem(name):
            return ctx.enter_context(nc.semaphore(name))

        wq = sb("wq", [PART, CHUNKS, PROJ])
        wk = sb("wk", [PART, CHUNKS, PROJ])
        wv = sb("wv", [PART, CHUNKS, PROJ])
        wo = sb("wo", [PROJ, DIM])
        w1T = sb("w1T", [PART, CHUNKS, DIM])
        w2T = sb("w2T", [PART, CHUNKS, DIM])
        b1 = sb("b1", [PART, CHUNKS])
        b2 = sb("b2", [PART, CHUNKS])
        ident = sb("ident", [PART, PART])
        head_rows = sb("head_rows", [PART, HEADS])
        shift_rows = sb("shift_rows", [PART, HEADS])
        ones_cols = sb("ones_cols", [KEYS, 2, 32])

        xT = [sb(f"xT{p}", [PART, CHUNKS, QUERIES]) for p in range(2)]
        keysT = [sb(f"keysT{p}", [PART, CHUNKS, KEYS]) for p in range(2)]
        keys = [sb(f"keys{p}", [KEYS, DIM]) for p in range(2)]

        kT = sb("kT", [PROJ, KEYS])
        k_blocks = sb("k_blocks", [PROJ, HEADS, KEYS], fp32r)
        k_shift = sb("k_shift", [PART, HEADS, KEYS])
        v_half = sb("v_half", [KEYS, HEADS, 32])
        qT_round = sb("qT_round", [PROJ, QUERIES], fp32r)
        qT_low = sb("qT_low", [PART, QUERIES])
        qT_high = sb("qT_high", [PART, QUERIES])
        neg_max = sb("neg_max", [PART, TILES, MAX_COLS])
        probs = sb("probs", [KEYS, HEADS, QUERIES])
        inv_sum = sb("inv_sum", [PROJ, QUERIES])
        attnT = sb("attnT", [PROJ, QUERIES])
        x1T = sb("x1T", [PART, CHUNKS, QUERIES])

        hT = sb("hT", [PART, CHUNKS, QUERIES])
        x2T = sb("x2T", [PART, CHUNKS, QUERIES])
        late_neg_max = sb("late_neg_max", [PART, TILES])
        late_probs = sb("late_probs", [PART, TILES, KEYS])
        late_sum = sb("late_sum", [PART, TILES])
        late_inv = sb("late_inv", [PART, TILES])
        late_norm = sb("late_norm", [PART, TILES, KEYS])
        late_probsT = sb("late_probsT", [KEYS, QUERIES])
        outT = sb("outT", [PART, CHUNKS, QUERIES])

        late = [bank(f"late{i}") for i in range(2)]
        early = [bank(f"early{i}") for i in range(4)]
        numer = bank("numer")
        denom = bank("denom")

        weights_loaded = sem("weights_loaded")
        kv_weights_loaded = sem("kv_weights_loaded")
        masks_loaded = sem("masks_loaded")
        x_loaded = [sem(f"x_loaded{p}") for p in range(2)]
        keysT_loaded = [sem(f"keysT_loaded{p}") for p in range(2)]
        keys_loaded = [sem(f"keys_loaded{p}") for p in range(2)]
        out_stored = sem("out_stored")
        pool_zeroed = sem("pool_zeroed")
        pool_ready = sem("pool_ready")
        dve_ready = sem("dve_ready")
        kv_mm = sem("kv_mm")
        kT_copied = sem("kT_copied")
        v_copied = sem("v_copied")
        k_built = sem("k_built")
        q_mm = sem("q_mm")
        q_rounded = sem("q_rounded")
        q_low = sem("q_low")
        q_high = sem("q_high")
        rank_mm = sem("rank_mm")
        max_done = sem("max_done")
        max_copied = sem("max_copied")
        maxT_mm = sem("maxT_mm")
        maxT_low = sem("maxT_low")
        maxT_high = sem("maxT_high")
        score_mm = sem("score_mm")
        exp_done = sem("exp_done")
        pv_mm = sem("pv_mm")
        inv_done = sem("inv_done")
        attn_done = sem("attn_done")
        wo_mm = sem("wo_mm")
        x1_done = sem("x1_done")
        up_mm = sem("up_mm")
        h_done = sem("h_done")
        down_mm = sem("down_mm")
        x2_done = sem("x2_done")
        late_score_mm = sem("late_score_mm")
        late_max_done = sem("late_max_done")
        late_exp_done = sem("late_exp_done")
        late_inv_done = sem("late_inv_done")
        late_norm_done = sem("late_norm_done")
        late_T_mm = sem("late_T_mm")
        late_T_copied = sem("late_T_copied")
        out_mm = sem("out_mm")
        out_done = sem("out_done")

        block = ctx.enter_context(nc.Block())

        def run_steps(engine, step):
            step(-1, 1, has_late=False)
            step(0, 0, first=True)
            with engine.Fori(0, BATCHES // 2 - 1) as pair:
                step(pair, 1)
                step(pair + 1, 0)
            step(BATCHES // 2 - 1, 1, has_early=False)

        @block.sync
        def _(sp):
            def load(b, p):
                sp.dma_start(keysT[p][:, :, :], ctxT_d[bass.ds(b, 1)].rearrange("o p c k -> p (o c) k")).then_inc(keysT_loaded[p], 16)
                sp.dma_start(xT[p][:, :, :], xT_d[bass.ds(b, 1)].rearrange("o p c q -> p (o c) q")).then_inc(x_loaded[p], 16)
                sp.dma_start(keys[p][:, :], ctx_d[bass.ds(b, 1)].rearrange("o k d -> k (o d)")).then_inc(keys_loaded[p], 16)

            sp.dma_start(head_rows[:, :], head_rows_d).then_inc(masks_loaded, 16)
            sp.dma_start(shift_rows[:, :], shift_rows_d).then_inc(masks_loaded, 16)
            sp.dma_start(wk[:, :, :], wk_d).then_inc(kv_weights_loaded, 16)
            sp.dma_start(wv[:, :, :], wv_d).then_inc(kv_weights_loaded, 16)
            sp.dma_start(wq[:, :, :], wq_d).then_inc(weights_loaded, 16)
            load(0, 0)
            sp.dma_start(ident[:, :], ident_d).then_inc(weights_loaded, 16)
            sp.dma_start(wo[:, :], wo_d).then_inc(weights_loaded, 16)
            sp.dma_start(b1[:, :], b1_d).then_inc(weights_loaded, 16)
            sp.dma_start(b2[:, :], b2_d).then_inc(weights_loaded, 16)
            sp.dma_start(w1T[:, :, :], w1T_d).then_inc(weights_loaded, 16)
            sp.dma_start(w2T[:, :, :], w2T_d).then_inc(weights_loaded, 16)
            load(1, 1)

            def step(pair, p, loads=True):
                b = 2 * pair + p
                if loads:
                    sp.wait_ge(x1_done, CHUNKS * b + CHUNKS)
                    sp.dma_start(xT[p][:, :, :], xT_d[bass.ds(b + 2, 1)].rearrange("o p c q -> p (o c) q")).then_inc(x_loaded[p], 16)
                    sp.wait_ge(late_score_mm, b + 1)
                    sp.dma_start(keysT[p][:, :, :], ctxT_d[bass.ds(b + 2, 1)].rearrange("o p c k -> p (o c) k")).then_inc(keysT_loaded[p], 16)
                for c in range(CHUNKS):
                    sp.wait_ge(out_done, CHUNKS * b + c + 1)
                    sp.dma_start(outT_d[bass.ds(b, 1), :, c, :].rearrange("o p q -> p (o q)"), outT[:, c, :]).then_inc(out_stored, 16)
                if loads:
                    sp.dma_start(keys[p][:, :], ctx_d[bass.ds(b + 2, 1)].rearrange("o k d -> k (o d)")).then_inc(keys_loaded[p], 16)

            step(0, 0)
            with sp.Fori(0, BATCHES // 2 - 2) as pair:
                step(pair, 1)
                step(pair + 1, 0)
            step(BATCHES // 2 - 2, 1)
            step(BATCHES // 2 - 1, 0, loads=False)
            step(BATCHES // 2 - 1, 1, loads=False)
            sp.wait_ge(out_stored, 16 * CHUNKS * BATCHES)

        @block.gpsimd
        def _(pool):
            nc.gpsimd.memset(v_half[:, :, :], 0.0)
            nc.gpsimd.memset(ones_cols[:, :, :], 0.0).then_inc(pool_zeroed, 1)
            pool.wait_ge(pool_zeroed, 1)
            nc.gpsimd.memset(ones_cols[:, 0, 0:16], 1.0)
            nc.gpsimd.memset(ones_cols[:, 1, 16:32], 1.0)
            pool.wait_ge(masks_loaded, 32)
            nc.gpsimd.tensor_copy(k_shift[:, :, :], shift_rows[:, :].unsqueeze(2).to_broadcast([PART, HEADS, KEYS])).then_inc(pool_ready, 1)
            pool.wait_ge(pool_ready, 1)

            def spread(out, rows, heads):
                n, h = rows.stop - rows.start, heads.stop - heads.start
                return nc.gpsimd.tensor_tensor(out[rows, heads, :], kT[rows, :].unsqueeze(1).to_broadcast([n, h, KEYS]),
                                               head_rows[rows, heads].unsqueeze(2).to_broadcast([n, h, KEYS]), MULT)

            def step(pair, p, has_late=True, has_early=True, first=False):
                if not has_early:
                    return
                a = 2 * pair + p + 1
                pool.wait_ge(kT_copied, a + 1)
                spread(k_blocks, slice(0, PART), slice(0, HEADS)).then_inc(k_built, 1)
                pool.wait_ge(k_built, 3 * a + 1)
                spread(k_shift, slice(0, LOW_ROWS), slice(0, LOW_HEADS)).then_inc(k_built, 1)
                pool.wait_ge(k_built, 3 * a + 2)
                spread(k_shift, slice(LOW_ROWS, PART), slice(LOW_HEADS, HEADS)).then_inc(k_built, 1)

            run_steps(pool, step)

        @block.scalar
        def _(act):
            act.wait_ge(weights_loaded, 16 * 7)
            act.wait_ge(pool_ready, 1)
            act.wait_ge(dve_ready, 1)

            def step(pair, p, has_late=True, has_early=True, first=False):
                b = 2 * pair + p
                a = b + 1

                def project_copies():
                    act.wait_ge(kv_mm, a + 1)
                    nc.scalar.copy(kT[:, :], numer[:, 0:KEYS]).then_inc(kT_copied, 1)
                    halves = numer[0:KEYS, PART:PART + PROJ].rearrange("k (h two d) -> k h two d", two=2, d=HEAD_DIM)
                    pairs = v_half[:, :, :].rearrange("k (h two) c -> k h two c", two=2)
                    nc.scalar.copy(pairs[:, :, 0, 0:HEAD_DIM], halves[:, :, 0, :])
                    nc.scalar.copy(pairs[:, :, 1, HEAD_DIM:2 * HEAD_DIM], halves[:, :, 1, :]).then_inc(v_copied, 1)
                    act.wait_ge(q_mm, a + 1)
                    nc.scalar.copy(qT_round[:, :], denom[:, :]).then_inc(q_rounded, 1)
                    nc.scalar.copy(qT_high[LOW_ROWS:PART, :], denom[LOW_ROWS:PART, :]).then_inc(q_high, 1)

                def relu(c):
                    act.wait_ge(up_mm, CHUNKS * b + c + 1)
                    nc.scalar.activation(hT[:, c, :], late[c % 2][:, :], ACT.Relu, bias=b1[:, c:c + 1]).then_inc(h_done, 1)

                def copy_maxT_high():
                    act.wait_ge(maxT_mm, a + 1)
                    nc.scalar.copy(qT_high[0:HEADS, :], numer[0:HEADS, :]).then_inc(maxT_high, 1)

                def exp(i):
                    act.wait_ge(score_mm, HEADS * a + i + 1)
                    nc.scalar.activation(probs[:, HEAD_ORDER[i], :], early[i % 4][0:KEYS, :], ACT.Exp, scale=SCALE).then_inc(exp_done, 1)

                def late_exps():
                    act.wait_ge(late_max_done, b + 1)
                    for t in range(TILES):
                        nc.scalar.activation(late_probs[:, t, :], late[0][:, t * KEYS:(t + 1) * KEYS], ACT.Exp,
                                             bias=late_neg_max[:, t:t + 1], accum_out=late_sum[:, t:t + 1]).then_inc(late_exp_done, 1)

                def copy_late_probsT():
                    act.wait_ge(late_T_mm, b + 1)
                    nc.scalar.copy(late_probsT[:, :], late[1][0:KEYS, :]).then_inc(late_T_copied, 1)

                if has_early:
                    project_copies()
                if has_late:
                    for c in range(CHUNKS):
                        relu(c)
                if has_early:
                    copy_maxT_high()
                    for i in range(6):
                        exp(i)
                if has_late:
                    late_exps()
                if has_early:
                    exp(6)
                    exp(7)
                if has_late:
                    copy_late_probsT()

            run_steps(act, step)

        @block.vector
        def _(dve):
            nc.vector.memset(neg_max[:, :, :], 0.0)
            nc.vector.memset(qT_low[:, :], 0.0)
            nc.vector.memset(qT_high[:, :], 0.0).then_inc(dve_ready, 1)
            dve.wait_ge(dve_ready, 1)
            dve.wait_ge(weights_loaded, 16 * 7)

            def step(pair, p, has_late=True, has_early=True, first=False):
                b = 2 * pair + p
                a = b + 1
                pa = 1 - p

                def copy_q_low():
                    dve.wait_ge(q_rounded, a + 1)
                    nc.vector.tensor_copy(qT_low[0:LOW_ROWS, :], denom[0:LOW_ROWS, :]).then_inc(q_low, 1)

                def maxima(i):
                    t, half = i // 2, i % 2
                    dve.wait_ge(rank_mm, HEADS * a + i + 1)
                    scores = early[i % 4][:, 0:HALF * KEYS].rearrange("q (h k) -> q h k", k=KEYS)
                    nc.vector.reduce_max(neg_max[:, t, HALF * half:HALF * (half + 1)], scores, AX.X, negate=True).then_inc(max_done, 1)

                def copy_maxima():
                    dve.wait_ge(max_done, HEADS * (a + 1))
                    nc.vector.tensor_copy(neg_max[:, :, LOW_ROWS:MAX_COLS], neg_max[:, :, 0:HEADS]).then_inc(max_copied, 1)

                def copy_maxT_low():
                    dve.wait_ge(maxT_mm, a + 1)
                    nc.vector.tensor_copy(qT_low[LOW_ROWS:MAX_COLS, :], numer[LOW_ROWS:MAX_COLS, :]).then_inc(maxT_low, 1)

                def x2(c):
                    dve.wait_ge(down_mm, CHUNKS * b + c + 1)
                    nc.vector.scalar_tensor_tensor(x2T[:, c, :], late[c % 2][:, :], b2[:, c:c + 1], x1T[:, c, :], ADD, ADD).then_inc(x2_done, 1)

                def late_maxima():
                    dve.wait_ge(late_score_mm, b + 1)
                    scores = late[0][:, 0:TILES * KEYS].rearrange("q (t k) -> q t k", k=KEYS)
                    nc.vector.reduce_max(late_neg_max[:, :], scores, AX.X, negate=True).then_inc(late_max_done, 1)

                def late_normalise():
                    dve.wait_ge(late_exp_done, TILES * (b + 1))
                    nc.vector.reciprocal(late_inv[:, :], late_sum[:, :]).then_inc(late_inv_done, 1)
                    dve.wait_ge(late_inv_done, b + 1)
                    nc.vector.tensor_tensor(late_norm[:, :, :], late_probs[:, :, :],
                                            late_inv[:, :].unsqueeze(2).to_broadcast([PART, TILES, KEYS]), MULT).then_inc(late_norm_done, 1)

                def normalise():
                    dve.wait_ge(pv_mm, a + 1)
                    nc.vector.reciprocal(inv_sum[:, :], denom[:, :]).then_inc(inv_done, 1)
                    dve.wait_ge(inv_done, a + 1)
                    nc.vector.tensor_tensor(attnT[:, :], numer[:, :], inv_sum[:, :], MULT).then_inc(attn_done, 1)

                def out(c):
                    dve.wait_ge(out_mm, CHUNKS * b + c + 1)
                    if c == 0 and not first:
                        dve.wait_ge(out_stored, 16 * CHUNKS * b)
                    nc.vector.tensor_tensor(outT[:, c, :], late[c % 2][:, :], x2T[:, c, :], ADD).then_inc(out_done, 1)

                def x1(c):
                    dve.wait_ge(wo_mm, CHUNKS * a + c + 1)
                    nc.vector.tensor_tensor(x1T[:, c, :], early[c][:, :], xT[pa][:, c, :], ADD).then_inc(x1_done, 1)

                if has_early:
                    copy_q_low()
                    for i in range(HEADS):
                        maxima(i)
                    copy_maxima()
                if has_late:
                    x2(0)
                if has_early:
                    copy_maxT_low()
                if has_late:
                    for c in range(1, CHUNKS):
                        x2(c)
                    late_maxima()
                    late_normalise()
                if has_early:
                    normalise()
                if has_late:
                    for c in range(CHUNKS):
                        out(c)
                if has_early:
                    for c in range(CHUNKS):
                        x1(c)

            run_steps(dve, step)

        @block.tensor
        def _(pe):
            def step(pair, p, has_late=True, has_early=True, first=False):
                b = 2 * pair + p
                a = b + 1
                pa, turn = 1 - p, pair + p

                def project_kv():
                    pe.wait_ge(keysT_loaded[pa], 16 * (turn + 1))
                    if not has_late:
                        pe.wait_ge(kv_weights_loaded, 32)
                    if has_late:
                        pe.wait_ge(attn_done, a)
                    for c in range(CHUNKS):
                        nc.tensor.matmul(numer[:, 0:KEYS], wk[:, c, :], keysT[pa][:, c, :], start=c == 0, stop=c == CHUNKS - 1)
                    for c in range(CHUNKS):
                        last = nc.tensor.matmul(numer[0:KEYS, PART:PART + PROJ], keysT[pa][:, c, :], wv[:, c, :],
                                                start=c == 0, stop=c == CHUNKS - 1)
                    last.then_inc(kv_mm, 1)

                def project_q():
                    pe.wait_ge(x_loaded[pa], 16 * (turn + 1))
                    if not has_late:
                        pe.wait_ge(weights_loaded, 16 * 7)
                    for c in range(CHUNKS):
                        last = nc.tensor.matmul(denom[:, :], wq[:, c, :], xT[pa][:, c, :], start=c == 0, stop=c == CHUNKS - 1)
                    last.then_inc(q_mm, 1)

                def rank(i):
                    t, half = i // 2, i % 2
                    if i == 0:
                        pe.wait_ge(k_built, 3 * a + 1)
                        pe.wait_ge(q_rounded, a + 1)
                    if i < 4 and has_late:
                        pe.wait_ge(x1_done, CHUNKS * a)
                    if i >= 4:
                        pe.wait_ge(max_done, HEADS * a + i - 3)
                    nc.tensor.matmul(early[i % 4][:, 0:HALF * KEYS], qT_round[:, t * PART:(t + 1) * PART],
                                     k_blocks[:, HALF * half:HALF * (half + 1), :], start=True, stop=True).then_inc(rank_mm, 1)

                def transpose_maxima():
                    pe.wait_ge(max_copied, a + 1)
                    pe.wait_ge(v_copied, a + 1)
                    for t in range(TILES):
                        last = nc.tensor.transpose(numer[0:MAX_COLS, t * PART:(t + 1) * PART], neg_max[:, t, :], ident[:, :])
                    last.then_inc(maxT_mm, 1)

                def score(i):
                    h = HEAD_ORDER[i]
                    if i == 0:
                        pe.wait_ge(k_built, 3 * a + 3)
                        pe.wait_ge(q_low, a + 1)
                        pe.wait_ge(q_high, a + 1)
                        pe.wait_ge(maxT_low, a + 1)
                        pe.wait_ge(maxT_high, a + 1)
                    if i >= 4:
                        pe.wait_ge(exp_done, HEADS * a + i - 3)
                    q = qT_low if h < LOW_HEADS else qT_high
                    nc.tensor.matmul(early[i % 4][0:KEYS, :], k_shift[:, h, :], q[:, :], start=True, stop=True).then_inc(score_mm, 1)

                def weigh_values(odd):
                    for j in range(HALF):
                        pe.wait_ge(exp_done, HEADS * a + HALF * odd + j + 1)
                        h, tile = 2 * j + odd, slice(32 * j, 32 * j + 32)
                        nc.tensor.matmul(numer[tile, :], v_half[:, h, :], probs[:, h, :], start=not odd, stop=bool(odd), tile_position=(0, 32 * j))
                    for j in range(HALF):
                        h, tile = 2 * j + odd, slice(32 * j, 32 * j + 32)
                        last = nc.tensor.matmul(denom[tile, :], ones_cols[:, odd, :], probs[:, h, :], start=not odd, stop=bool(odd), tile_position=(0, 32 * j))
                    if odd:
                        last.then_inc(pv_mm, 1)

                def project_out(c):
                    if c == 0:
                        pe.wait_ge(attn_done, a + 1)
                    nc.tensor.matmul(early[c][:, :], wo[:, c * PART:(c + 1) * PART], attnT[:, :], start=True, stop=True).then_inc(wo_mm, 1)

                def up(f):
                    if f < 2 and not first:
                        pe.wait_ge(out_done, CHUNKS * b)
                    if f == 0:
                        pe.wait_ge(x1_done, CHUNKS * (b + 1))
                    if f >= 2:
                        pe.wait_ge(h_done, CHUNKS * b + f - 1)
                    for c in range(CHUNKS):
                        last = nc.tensor.matmul(late[f % 2][:, :], w1T[:, c, f * PART:(f + 1) * PART], x1T[:, c, :],
                                                start=c == 0, stop=c == CHUNKS - 1)
                    last.then_inc(up_mm, 1)

                def down(d):
                    if d < 2:
                        pe.wait_ge(h_done, CHUNKS * (b + 1))
                    else:
                        pe.wait_ge(x2_done, CHUNKS * b + d - 1)
                    for c in range(CHUNKS):
                        last = nc.tensor.matmul(late[d % 2][:, :], w2T[:, c, d * PART:(d + 1) * PART], hT[:, c, :],
                                                start=c == 0, stop=c == CHUNKS - 1)
                    last.then_inc(down_mm, 1)

                def late_scores():
                    pe.wait_ge(x2_done, CHUNKS * (b + 1))
                    for t in range(TILES):
                        for c in range(CHUNKS):
                            last = nc.tensor.matmul(late[0][:, t * KEYS:(t + 1) * KEYS], x2T[:, c, t * PART:(t + 1) * PART],
                                                    keysT[p][:, c, :], start=c == 0, stop=c == CHUNKS - 1)
                    last.then_inc(late_score_mm, 1)

                def late_transpose():
                    pe.wait_ge(late_norm_done, b + 1)
                    for t in range(TILES):
                        last = nc.tensor.transpose(late[1][0:KEYS, t * PART:(t + 1) * PART], late_norm[:, t, :], ident[:, :])
                    last.then_inc(late_T_mm, 1)

                def output(c):
                    if c == 0:
                        pe.wait_ge(late_T_copied, b + 1)
                        pe.wait_ge(keys_loaded[p], 16 * (pair + 1))
                    if c >= 2:
                        pe.wait_ge(out_done, CHUNKS * b + c - 1)
                    nc.tensor.matmul(late[c % 2][:, :], keys[p][:, c * PART:(c + 1) * PART], late_probsT[:, :],
                                     start=True, stop=True).then_inc(out_mm, 1)

                if has_early:
                    project_kv()
                    project_q()
                if has_late:
                    up(0)
                    up(1)
                if has_early:
                    for i in range(4):
                        rank(i)
                if has_late:
                    up(2)
                if has_early:
                    rank(4)
                    rank(5)
                if has_late:
                    up(3)
                if has_early:
                    rank(6)
                    rank(7)
                if has_late:
                    down(0)
                if has_early:
                    transpose_maxima()
                if has_late:
                    down(1)
                if has_early:
                    score(0)
                    score(1)
                if has_late:
                    down(2)
                if has_early:
                    score(2)
                    score(3)
                if has_late:
                    down(3)
                if has_early:
                    score(4)
                    score(5)
                if has_late:
                    late_scores()
                if has_early:
                    score(6)
                    score(7)
                    weigh_values(0)
                    weigh_values(1)
                if has_late:
                    late_transpose()
                    for c in range(CHUNKS):
                        output(c)
                if has_early:
                    for c in range(CHUNKS):
                        project_out(c)

            run_steps(pe, step)


def kernel(x, ctx_1024, L0_xattn_W_q, L0_xattn_W_k, L0_xattn_W_v, L0_xattn_W_o,
           L0_xattn_w1, L0_xattn_b1, L0_xattn_w2, L0_xattn_b2):
    import numpy as np
    import concourse.bacc as bacc
    from concourse.bass_utils import run_bass_kernel_spmd

    def by_partition(w):
        w = np.asarray(w)
        return w.reshape(CHUNKS, PART, w.shape[1]).transpose(1, 0, 2)

    x, ctx = np.asarray(x), np.asarray(ctx_1024)
    row, head = np.arange(PART)[:, None], np.arange(HEADS)[None, :]
    shift = np.where(head < LOW_HEADS, row == LOW_ROWS + head, row == head)
    inputs = {
        "xT": x.reshape(BATCHES, QUERIES, CHUNKS, PART).transpose(0, 3, 2, 1),
        "ctx": ctx,
        "ctxT": ctx.reshape(BATCHES, KEYS, CHUNKS, PART).transpose(0, 3, 2, 1),
        "wq": by_partition(L0_xattn_W_q),
        "wk": by_partition(L0_xattn_W_k),
        "wv": by_partition(L0_xattn_W_v),
        "wo": np.asarray(L0_xattn_W_o),
        "w1T": by_partition(np.asarray(L0_xattn_w1).T),
        "b1": np.asarray(L0_xattn_b1).reshape(CHUNKS, PART).T,
        "w2T": by_partition(np.asarray(L0_xattn_w2).T),
        "b2": np.asarray(L0_xattn_b2).reshape(CHUNKS, PART).T,
        "ident": np.eye(PART, dtype=np.float32),
        "head_rows": (row // HEAD_DIM == head).astype(np.float32),
        "shift_rows": shift.astype(np.float32),
    }
    inputs = {name + "_dram": np.ascontiguousarray(a) for name, a in inputs.items()}
    nc = bacc.Bacc("TRN2", target_bir_lowering=False, num_devices=1)
    args = [nc.dram_tensor(name, a.shape, mybir.dt.from_np(a.dtype), kind="ExternalInput").ap()
            for name, a in inputs.items()]
    outT = nc.dram_tensor("outT_dram", (BATCHES, PART, CHUNKS, QUERIES), mybir.dt.float32, kind="ExternalOutput").ap()
    cross_attention_ffn_attention(nc, *args, outT)
    result = run_bass_kernel_spmd(nc, [inputs], core_ids=[0]).results[0]["outT_dram"]
    return np.ascontiguousarray(result.transpose(0, 3, 2, 1)).reshape(BATCHES, QUERIES, DIM)
```

```python
import concourse.bass as bass
from concourse import mybir
from concourse.alu_op_type import AluOpType
from contextlib import ExitStack

BATCHES, QUERIES, DIM, KEYS = 16, 512, 512, 120
HEADS, HEAD_DIM = 8, 16
PART = 128
CHUNKS = DIM // PART
TILES = QUERIES // PART
PROJ = HEADS * HEAD_DIM
HALF = HEADS // 2
SCALE = HEAD_DIM ** -0.5
PAIRS = HEADS // 2
PAIR_ROWS = 2 * HEAD_DIM
HALVES = [slice(0, QUERIES // 2), slice(QUERIES // 2, QUERIES)]
SWAP_HEADS = [(r + HEAD_DIM) % PAIR_ROWS for r in range(PAIR_ROWS)]
STACK = 3 * PAIR_ROWS
STACK_MAX = STACK + HEADS
HEAD_ORDER = [0, 2, 4, 6, 1, 3, 5, 7]


def cross_attention_ffn_attention(nc, xT_d, ctx_d, ctxT_d, wq_d, wk_d, wv_d, wo_d, w1T_d, b1_d, w2T_d, b2_d,
                                  ident_d, pair_rows_d, max_rows_d, outT_d):
    fp32, fp32r = mybir.dt.float32, mybir.dt.float32r
    ACT, AX = mybir.ActivationFunctionType, mybir.AxisListType
    ADD, SUB, MULT = AluOpType.add, AluOpType.subtract, AluOpType.mult

    with ExitStack() as ctx:
        def sb(name, shape, dt=fp32):
            return ctx.enter_context(nc.sbuf_tensor(name, shape, dt))

        def bank(name):
            return ctx.enter_context(nc.psum_tensor(name, [PART, 512], fp32))

        def sem(name):
            return ctx.enter_context(nc.semaphore(name))

        def split(name, shape):
            return sb(name + "_hi", shape, fp32r), sb(name + "_lo", shape, fp32r)

        wk = sb("wk", [PART, CHUNKS, PROJ])
        wv = sb("wv", [PART, CHUNKS, PROJ])
        wq = sb("wq", [PART, CHUNKS, PROJ])
        wo = sb("wo", [PROJ, DIM])
        wq_hi, wq_lo = split("wq", [PART, CHUNKS, PROJ])
        wo_hi, wo_lo = split("wo", [PROJ, DIM])
        w1T_hi, w1T_lo = split("w1T", [PART, CHUNKS, DIM])
        w2T_hi, w2T_lo = split("w2T", [PART, CHUNKS, DIM])
        b1 = sb("b1", [PART, CHUNKS])
        b2 = sb("b2", [PART, CHUNKS])
        ident = sb("ident", [PART, PART])
        pair_rows = sb("pair_rows", [PART, 2])
        max_rows = sb("max_rows", [PART, HEADS])

        xT = [sb(f"xT{p}", [PART, CHUNKS, QUERIES]) for p in range(2)]
        early_keysT = sb("early_keysT", [PART, CHUNKS, KEYS])
        late_keysT = sb("late_keysT", [PART, CHUNKS, KEYS])
        keys = [sb(f"keys{p}", [KEYS, DIM]) for p in range(2)]
        xT_hi, xT_lo = split("xT", [PART, CHUNKS, QUERIES])
        keys_hi, keys_lo = split("keys", [KEYS, DIM])

        k_parts = sb("k_parts", [STACK, PAIRS, KEYS], fp32r)
        k_stack = sb("k_stack", [PART, HEADS, KEYS], fp32r)
        v_ones = sb("v_ones", [KEYS, HEADS, PAIR_ROWS])
        q_stack = sb("q_stack", [PART, PAIRS, QUERIES], fp32r)
        neg_max = sb("neg_max", [PART, TILES, STACK_MAX])
        probs = sb("probs", [KEYS, HEADS, QUERIES])
        even_numer = sb("even_numer", [PROJ, QUERIES])
        even_sum = sb("even_sum", [PROJ, QUERIES])
        swapped_sum = sb("swapped_sum", [PROJ, QUERIES])
        inv_sum = sb("inv_sum", [PROJ, QUERIES])
        attnT = sb("attnT", [PROJ, QUERIES])
        attnT_hi, attnT_lo = split("attnT", [PROJ, QUERIES])
        x1T = sb("x1T", [PART, CHUNKS, QUERIES])
        x1T_hi, x1T_lo = split("x1T", [PART, CHUNKS, QUERIES])

        hT = sb("hT", [PART, 2, QUERIES])
        hT_hi, hT_lo = split("hT", [PART, CHUNKS, QUERIES])
        x2T = sb("x2T", [PART, CHUNKS, QUERIES])
        late_neg_max = sb("late_neg_max", [PART, TILES])
        late_probs = sb("late_probs", [PART, TILES, KEYS])
        late_sum = sb("late_sum", [PART, TILES])
        late_inv = sb("late_inv", [PART, TILES])
        late_norm = sb("late_norm", [PART, TILES, KEYS])
        late_probsT_hi, late_probsT_lo = split("late_probsT", [KEYS, QUERIES])
        outT = sb("outT", [PART, CHUNKS, QUERIES])
        w1T, w2T = x2T, outT

        late = [bank(f"late{i}") for i in range(2)]
        early = [bank(f"early{i}") for i in range(4)]
        evens = bank("evens")
        odds = bank("odds")

        out_banks = [late[0], late[1], early[2], early[3]]

        masks_loaded = sem("masks_loaded")
        kv_weights_loaded = sem("kv_weights_loaded")
        wq_loaded = sem("wq_loaded")
        small_loaded = sem("small_loaded")
        ffn_loaded = sem("ffn_loaded")
        first_x_loaded = [sem(f"first_x_loaded{c}") for c in range(CHUNKS)]
        x_loaded = [sem(f"x_loaded{p}") for p in range(2)]
        early_keysT_loaded = sem("early_keysT_loaded")
        late_keysT_loaded = sem("late_keysT_loaded")
        keys_loaded = [sem(f"keys_loaded{p}") for p in range(2)]
        out_stored = sem("out_stored")
        ones_set = sem("ones_set")
        pool_ready = sem("pool_ready")
        dve_ready = sem("dve_ready")
        wq_split = sem("wq_split")
        wo_split = sem("wo_split")
        w1_split = sem("w1_split")
        w2_split = sem("w2_split")
        first_x_rounded = sem("first_x_rounded")
        x_rounded = sem("x_rounded")
        first_x_split = sem("first_x_split")
        x_split = sem("x_split")
        k_mm = sem("k_mm")
        v_mm = sem("v_mm")
        k_rounded = sem("k_rounded")
        k_split = sem("k_split")
        v_copied = sem("v_copied")
        k_built = sem("k_built")
        q_mm = sem("q_mm")
        q_rounded = sem("q_rounded")
        q_split = sem("q_split")
        q_stacked = sem("q_stacked")
        rank_mm = sem("rank_mm")
        max_done = sem("max_done")
        maxT_mm = sem("maxT_mm")
        max_stacked = sem("max_stacked")
        score_mm = sem("score_mm")
        exp_done = sem("exp_done")
        pv_mm = sem("pv_mm")
        even_sum_done = sem("even_sum_done")
        even_numer_done = sem("even_numer_done")
        sum_swapped = sem("sum_swapped")
        numer_done = sem("numer_done")
        inv_swapped = sem("inv_swapped")
        inv_done = sem("inv_done")
        attn_done = sem("attn_done")
        attn_rounded = sem("attn_rounded")
        attn_split = sem("attn_split")
        wo_mm = sem("wo_mm")
        x1_done = sem("x1_done")
        x1_rounded = sem("x1_rounded")
        x1_split = sem("x1_split")
        up_mm = sem("up_mm")
        h_rounded = sem("h_rounded")
        h_split = sem("h_split")
        down_mm = sem("down_mm")
        x2_done = sem("x2_done")
        late_score_mm = sem("late_score_mm")
        late_max_done = sem("late_max_done")
        late_exp_done = sem("late_exp_done")
        late_inv_done = sem("late_inv_done")
        late_norm_done = sem("late_norm_done")
        late_T_mm = sem("late_T_mm")
        late_T_rounded = sem("late_T_rounded")
        late_T_split = sem("late_T_split")
        keys_rounded = sem("keys_rounded")
        keys_split = sem("keys_split")
        out_mm = sem("out_mm")
        out_done = sem("out_done")

        block = ctx.enter_context(nc.Block())

        def run_steps(engine, step):
            step(-1, 1, has_late=False)
            step(0, 0, first=True)
            with engine.Fori(0, BATCHES // 2 - 2) as pair:
                step(pair, 1)
                step(pair + 1, 0)
            step(BATCHES // 2 - 2, 1)
            step(BATCHES // 2 - 1, 0, has_next=False)
            step(BATCHES // 2 - 1, 1, has_early=False)

        @block.sync
        def _(sp):
            def load_x(b, p):
                sp.dma_start(xT[p][:, :, :], xT_d[bass.ds(b, 1)].rearrange("o p c q -> p (o c) q")).then_inc(x_loaded[p], 16)

            def load_early_keysT(b):
                sp.dma_start(early_keysT[:, :, :], ctxT_d[bass.ds(b, 1)].rearrange("o p c k -> p (o c) k")).then_inc(early_keysT_loaded, 16)

            def load_late_keysT(b):
                sp.dma_start(late_keysT[:, :, :], ctxT_d[bass.ds(b, 1)].rearrange("o p c k -> p (o c) k")).then_inc(late_keysT_loaded, 16)

            def load_keys(b, p):
                sp.dma_start(keys[p][:, :], ctx_d[bass.ds(b, 1)].rearrange("o k d -> k (o d)")).then_inc(keys_loaded[p], 16)

            sp.dma_start(wk[:, :, :], wk_d).then_inc(kv_weights_loaded, 16)
            load_early_keysT(0)
            sp.dma_start(wv[:, :, :], wv_d).then_inc(kv_weights_loaded, 16)
            sp.dma_start(wq[:, :, :], wq_d).then_inc(wq_loaded, 16)
            for c in range(CHUNKS):
                sp.dma_start(xT[0][:, c, :], xT_d[0, :, c, :]).then_inc(first_x_loaded[c], 16)
            sp.dma_start(pair_rows[:, :], pair_rows_d).then_inc(masks_loaded, 16)
            sp.dma_start(max_rows[:, :], max_rows_d).then_inc(masks_loaded, 16)
            sp.dma_start(ident[:, :], ident_d).then_inc(small_loaded, 16)
            sp.dma_start(wo[:, :], wo_d).then_inc(small_loaded, 16)
            sp.dma_start(b1[:, :], b1_d).then_inc(small_loaded, 16)
            sp.dma_start(b2[:, :], b2_d).then_inc(small_loaded, 16)
            load_x(1, 1)
            sp.dma_start(w1T[:, :, :], w1T_d).then_inc(ffn_loaded, 16)
            sp.wait_ge(v_mm, 1)
            load_early_keysT(1)
            load_late_keysT(0)
            sp.dma_start(w2T[:, :, :], w2T_d).then_inc(ffn_loaded, 16)
            load_keys(0, 0)
            load_keys(1, 1)

            def step(pair, p, loads=True, last=False):
                b = 2 * pair + p
                if loads:
                    sp.wait_ge(v_mm, b + 2)
                    load_early_keysT(b + 2)
                    sp.wait_ge(x1_done, CHUNKS * b + CHUNKS)
                    load_x(b + 2, p)
                if not last:
                    sp.wait_ge(late_score_mm, b + 1)
                    load_late_keysT(b + 1)
                for c in range(CHUNKS):
                    sp.wait_ge(out_done, CHUNKS * b + c + 1)
                    sp.dma_start(outT_d[bass.ds(b, 1), :, c, :].rearrange("o p q -> p (o q)"), outT[:, c, :]).then_inc(out_stored, 16)
                if loads:
                    load_keys(b + 2, p)

            step(0, 0)
            with sp.Fori(0, BATCHES // 2 - 2) as pair:
                step(pair, 1)
                step(pair + 1, 0)
            step(BATCHES // 2 - 2, 1)
            step(BATCHES // 2 - 1, 0, loads=False)
            step(BATCHES // 2 - 1, 1, loads=False, last=True)
            sp.wait_ge(out_stored, 16 * CHUNKS * BATCHES)

        @block.gpsimd
        def _(pool):
            nc.gpsimd.memset(v_ones[:, :, :], 1.0).then_inc(ones_set, 1)
            pool.wait_ge(masks_loaded, 32)
            nc.gpsimd.tensor_copy(k_stack[:, :, :], max_rows[:, :].unsqueeze(2).to_broadcast([PART, HEADS, KEYS])).then_inc(pool_ready, 1)
            pool.wait_ge(pool_ready, 1)

            def build_k(n):
                pool.wait_ge(k_split, n + 1)
                stack = k_stack[0:STACK, :, :].rearrange("r (pair odd) k -> r pair odd k", odd=2)
                for odd in range(2):
                    rows = pair_rows[0:STACK, odd:odd + 1].unsqueeze(2).to_broadcast([STACK, PAIRS, KEYS])
                    nc.gpsimd.tensor_tensor(stack[:, :, odd, :], k_parts[:, :, :].bitcast(fp32), rows, MULT).then_inc(k_built, 1)
                    pool.wait_ge(k_built, 2 * n + odd + 1)

            build_k(0)

            def split_x(n, p):
                pool.wait_ge(x_rounded, n)
                nc.gpsimd.tensor_tensor(xT_lo[:, :, :], xT[p][:, :, :], xT_hi[:, :, :].bitcast(fp32), SUB).then_inc(x_split, 1)
                pool.wait_ge(x_split, n)

            def step(pair, p, has_late=True, has_early=True, first=False, has_next=True):
                b = 2 * pair + p
                a = b + 1
                if has_early and has_next:
                    split_x(a + 1, p)
                if not has_late:
                    pool.wait_ge(ffn_loaded, 32)
                    nc.gpsimd.tensor_copy(w2T_hi[:, :, :], w2T[:, :, :]).then_inc(w2_split, 1)
                    pool.wait_ge(w2_split, 1)
                    nc.gpsimd.tensor_tensor(w2T_lo[:, :, :], w2T[:, :, :], w2T_hi[:, :, :].bitcast(fp32), SUB).then_inc(w2_split, 1)
                    pool.wait_ge(w2_split, 2)
                if has_late:
                    pool.wait_ge(keys_rounded, b + 1)
                    nc.gpsimd.tensor_tensor(keys_lo[:, :], keys[p][:, :], keys_hi[:, :].bitcast(fp32), SUB).then_inc(keys_split, 1)
                    pool.wait_ge(keys_split, b + 1)
                if has_early:
                    for c in range(CHUNKS):
                        pool.wait_ge(x1_rounded, CHUNKS * a + c + 1)
                        nc.gpsimd.tensor_tensor(x1T_lo[:, c, :], x1T[:, c, :], x1T_hi[:, c, :].bitcast(fp32), SUB).then_inc(x1_split, 1)
                    pool.wait_ge(x1_split, CHUNKS * (a + 1))
                if has_early and has_next:
                    build_k(a + 1)

            run_steps(pool, step)

        @block.scalar
        def _(act):
            def round_k(n):
                act.wait_ge(k_mm, n + 1)
                for pair_ in range(PAIRS):
                    last = nc.scalar.copy(k_parts[0:PAIR_ROWS, pair_, :], evens[PAIR_ROWS * pair_:PAIR_ROWS * (pair_ + 1), 0:KEYS])
                last.then_inc(k_rounded, 1)

            def copy_v(n, first_batch=False):
                act.wait_ge(v_mm, n + 1)
                if not first_batch:
                    act.wait_ge(pv_mm, 2 * n)
                halves = early[0][0:KEYS, 0:PROJ].rearrange("k (pair odd d) -> k pair odd d", odd=2, d=HEAD_DIM)
                pairs = v_ones[:, :, :].rearrange("k (pair odd) c -> k pair odd c", odd=2)
                nc.scalar.copy(pairs[:, :, 0, 0:HEAD_DIM], halves[:, :, 0, :])
                nc.scalar.copy(pairs[:, :, 1, HEAD_DIM:2 * HEAD_DIM], halves[:, :, 1, :]).then_inc(v_copied, 1)

            def stack_q(n):
                act.wait_ge(q_mm, n + 1)
                for half in range(2):
                    for pair_ in range(2 * half, 2 * half + 2):
                        nc.scalar.copy(q_stack[0:PAIR_ROWS, pair_, :], odds[PAIR_ROWS * pair_:PAIR_ROWS * (pair_ + 1), :]).then_inc(q_rounded, 1)
                    act.wait_ge(q_rounded, PAIRS * n + 2 * half + 2)
                    nc.scalar.copy(q_stack[2 * PAIR_ROWS:STACK, 2 * half:2 * half + 2, :],
                                   q_stack[0:PAIR_ROWS, 2 * half:2 * half + 2, :].bitcast(fp32)).then_inc(q_stacked, 1)

            act.wait_ge(wq_loaded, 16)
            nc.scalar.copy(wq_hi[:, :, :], wq[:, :, :]).then_inc(wq_split, 1)
            for c in range(CHUNKS):
                act.wait_ge(first_x_loaded[c], 16)
                nc.scalar.copy(xT_hi[:, c, :], xT[0][:, c, :]).then_inc(first_x_rounded, 1)
            act.wait_ge(ones_set, 1)
            act.wait_ge(masks_loaded, 32)
            round_k(0)
            copy_v(0, first_batch=True)
            stack_q(0)

            def step(pair, p, has_late=True, has_early=True, first=False, has_next=True):
                b = 2 * pair + p
                a = b + 1

                def relu(c):
                    act.wait_ge(up_mm, CHUNKS * b + c + 1)
                    if first and c == 0:
                        act.wait_ge(small_loaded, 16 * 4)
                    if c >= 2 or not first:
                        act.wait_ge(h_split, CHUNKS * b + c - 1)
                    nc.scalar.activation(hT[:, c % 2, :], late[c % 2][:, :], ACT.Relu, bias=b1[:, c:c + 1])
                    nc.scalar.activation(hT_hi[:, c, :], late[c % 2][:, :], ACT.Relu, bias=b1[:, c:c + 1]).then_inc(h_rounded, 1)

                def stack_maxima():
                    act.wait_ge(maxT_mm, a + 1)
                    for half in range(2):
                        nc.scalar.copy(q_stack[STACK:STACK_MAX, 2 * half:2 * half + 2, :],
                                       evens[STACK:STACK_MAX, :].unsqueeze(1).to_broadcast([HEADS, 2, QUERIES])).then_inc(max_stacked, 1)

                def exp(i):
                    act.wait_ge(score_mm, HEADS * a + i + 1)
                    nc.scalar.activation(probs[:, HEAD_ORDER[i], :], early[i % 4][0:KEYS, :], ACT.Exp, scale=SCALE).then_inc(exp_done, 1)

                def late_exps():
                    act.wait_ge(late_max_done, b + 1)
                    for t in range(TILES):
                        nc.scalar.activation(late_probs[:, t, :], late[0][:, t * KEYS:(t + 1) * KEYS], ACT.Exp,
                                             bias=late_neg_max[:, t:t + 1], accum_out=late_sum[:, t:t + 1]).then_inc(late_exp_done, 1)

                def round_late_probsT():
                    act.wait_ge(late_T_mm, b + 1)
                    nc.scalar.copy(late_probsT_hi[:, :], late[1][0:KEYS, :]).then_inc(late_T_rounded, 1)

                def part_evens():
                    act.wait_ge(pv_mm, 2 * a + 1)
                    nc.scalar.activation(even_sum[:, :], evens[:, :], ACT.Identity, scale=pair_rows[:, 1:2]).then_inc(even_sum_done, 1)
                    nc.scalar.activation(even_numer[:, :], evens[:, :], ACT.Identity, scale=pair_rows[:, 0:1]).then_inc(even_numer_done, 1)

                def round_attn(half):
                    act.wait_ge(attn_done, 2 * a + half + 1)
                    nc.scalar.copy(attnT_hi[:, HALVES[half]], attnT[:, HALVES[half]]).then_inc(attn_rounded, 1)

                def round_x1(c):
                    act.wait_ge(x1_done, CHUNKS * a + c + 1)
                    nc.scalar.copy(x1T_hi[:, c, :], x1T[:, c, :]).then_inc(x1_rounded, 1)

                if has_late:
                    for c in range(3):
                        relu(c)
                if has_early:
                    stack_maxima()
                if has_late:
                    relu(3)
                if has_early:
                    for i in range(HEADS):
                        exp(i)
                    part_evens()
                    round_attn(0)
                    round_attn(1)
                if has_late:
                    late_exps()
                if has_early:
                    round_x1(0)
                    round_x1(1)
                if has_late:
                    round_late_probsT()
                if has_early:
                    round_x1(2)
                    round_x1(3)
                if has_early and has_next:
                    round_k(a + 1)
                    copy_v(a + 1)
                    stack_q(a + 1)

            run_steps(act, step)

        @block.vector
        def _(dve):
            nc.vector.memset(neg_max[:, :, :], 0.0).then_inc(dve_ready, 1)
            dve.wait_ge(dve_ready, 1)
            dve.wait_ge(wq_split, 1)
            nc.vector.tensor_tensor(wq_lo[:, :, :], wq[:, :, :], wq_hi[:, :, :].bitcast(fp32), SUB).then_inc(wq_split, 1)
            for c in range(CHUNKS):
                dve.wait_ge(first_x_rounded, c + 1)
                nc.vector.tensor_tensor(xT_lo[:, c, :], xT[0][:, c, :], xT_hi[:, c, :].bitcast(fp32), SUB).then_inc(first_x_split, 1)

            def split_wo():
                dve.wait_ge(small_loaded, 16 * 4)
                nc.vector.tensor_copy(wo_hi[:, :], wo[:, :]).then_inc(wo_split, 1)
                dve.wait_ge(wo_split, 1)
                nc.vector.tensor_tensor(wo_lo[:, :], wo[:, :], wo_hi[:, :].bitcast(fp32), SUB).then_inc(wo_split, 1)

            def split_k(n):
                dve.wait_ge(k_rounded, n + 1)
                for pair_ in range(PAIRS):
                    nc.vector.tensor_tensor(k_parts[2 * PAIR_ROWS:STACK, pair_, :], evens[PAIR_ROWS * pair_:PAIR_ROWS * (pair_ + 1), 0:KEYS],
                                            k_parts[0:PAIR_ROWS, pair_, :].bitcast(fp32), SUB)
                nc.vector.tensor_copy(k_parts[PAIR_ROWS:2 * PAIR_ROWS, :, :].bitcast(fp32),
                                      k_parts[0:PAIR_ROWS, :, :].bitcast(fp32)).then_inc(k_split, 1)

            def split_q(n):
                for pair_ in range(PAIRS):
                    dve.wait_ge(q_rounded, PAIRS * n + pair_ + 1)
                    nc.vector.tensor_tensor(q_stack[PAIR_ROWS:2 * PAIR_ROWS, pair_, :], odds[PAIR_ROWS * pair_:PAIR_ROWS * (pair_ + 1), :],
                                            q_stack[0:PAIR_ROWS, pair_, :].bitcast(fp32), SUB).then_inc(q_split, 1)

            split_k(0)
            split_q(0)

            def step(pair, p, has_late=True, has_early=True, first=False, has_next=True):
                b = 2 * pair + p
                a = b + 1
                pa = 1 - p

                def round_x():
                    dve.wait_ge(x_loaded[p], 16 * (pair + 1 + p))
                    nc.vector.tensor_copy(xT_hi[:, :, :], xT[p][:, :, :]).then_inc(x_rounded, 1)

                def split_w1():
                    dve.wait_ge(ffn_loaded, 32)
                    nc.vector.tensor_copy(w1T_hi[:, :, :], w1T[:, :, :]).then_inc(w1_split, 1)
                    dve.wait_ge(w1_split, 1)
                    nc.vector.tensor_tensor(w1T_lo[:, :, :], w1T[:, :, :], w1T_hi[:, :, :].bitcast(fp32), SUB).then_inc(w1_split, 1)

                def round_keys():
                    dve.wait_ge(keys_loaded[p], 16 * (pair + 1))
                    nc.vector.tensor_copy(keys_hi[:, :], keys[p][:, :]).then_inc(keys_rounded, 1)

                def maxima(i):
                    t, half = i % TILES, i // TILES
                    dve.wait_ge(rank_mm, HEADS * a + i + 1)
                    scores = early[i % 4][:, 0:HALF * KEYS].rearrange("q (h k) -> q h k", k=KEYS)
                    at = STACK + HALF * half
                    nc.vector.reduce_max(neg_max[:, t, at:at + HALF], scores, AX.X, negate=True).then_inc(max_done, 1)

                def split_h(c):
                    dve.wait_ge(h_rounded, CHUNKS * b + c + 1)
                    nc.vector.tensor_tensor(hT_lo[:, c, :], hT[:, c % 2, :], hT_hi[:, c, :].bitcast(fp32), SUB).then_inc(h_split, 1)

                def x2(c):
                    dve.wait_ge(down_mm, CHUNKS * b + c + 1)
                    nc.vector.scalar_tensor_tensor(x2T[:, c, :], late[c % 2][:, :], b2[:, c:c + 1], x1T[:, c, :], ADD, ADD).then_inc(x2_done, 1)

                def late_maxima():
                    dve.wait_ge(late_score_mm, b + 1)
                    scores = late[0][:, 0:TILES * KEYS].rearrange("q (t k) -> q t k", k=KEYS)
                    nc.vector.reduce_max(late_neg_max[:, :], scores, AX.X, negate=True).then_inc(late_max_done, 1)

                def late_normalise():
                    dve.wait_ge(late_exp_done, TILES * (b + 1))
                    nc.vector.reciprocal(late_inv[:, :], late_sum[:, :]).then_inc(late_inv_done, 1)
                    dve.wait_ge(late_inv_done, b + 1)
                    nc.vector.tensor_tensor(late_norm[:, :, :], late_probs[:, :, :],
                                            late_inv[:, :].unsqueeze(2).to_broadcast([PART, TILES, KEYS]), MULT).then_inc(late_norm_done, 1)

                def split_late_probsT():
                    dve.wait_ge(late_T_rounded, b + 1)
                    nc.vector.tensor_tensor(late_probsT_lo[:, :], late[1][0:KEYS, :], late_probsT_hi[:, :].bitcast(fp32), SUB).then_inc(late_T_split, 1)

                def merge_heads():
                    dve.wait_ge(pv_mm, 2 * a + 2)
                    dve.wait_ge(even_sum_done, a + 1)
                    nc.vector.scalar_tensor_tensor(swapped_sum[:, :], odds[:, :], pair_rows[:, 0:1], even_sum[:, :], MULT, ADD).then_inc(sum_swapped, 1)
                    dve.wait_ge(even_numer_done, a + 1)
                    nc.vector.scalar_tensor_tensor(attnT[:, :], odds[:, :], pair_rows[:, 1:2], even_numer[:, :], MULT, ADD).then_inc(numer_done, 1)
                    dve.wait_ge(sum_swapped, a + 1)

                def invert(half):
                    if half == 0:
                        dve.wait_ge(sum_swapped, a + 1)
                    else:
                        dve.wait_ge(inv_swapped, 2 * a + 1)
                    nc.vector.reciprocal(swapped_sum[:, HALVES[half]], swapped_sum[:, HALVES[half]]).then_inc(inv_swapped, 1)

                def swap_inverses(half):
                    nc.vector.stream_shuffle(inv_sum[:, HALVES[half]], swapped_sum[:, HALVES[half]], SWAP_HEADS).then_inc(inv_done, 1)

                def divide(half):
                    if half == 0:
                        dve.wait_ge(numer_done, a + 1)
                        dve.wait_ge(inv_swapped, 2 * a + 2)
                    dve.wait_ge(inv_done, 2 * a + half + 1)
                    nc.vector.tensor_tensor(attnT[:, HALVES[half]], attnT[:, HALVES[half]], inv_sum[:, HALVES[half]], MULT).then_inc(attn_done, 1)

                def split_attn(half):
                    dve.wait_ge(attn_rounded, 2 * a + half + 1)
                    nc.vector.tensor_tensor(attnT_lo[:, HALVES[half]], attnT[:, HALVES[half]], attnT_hi[:, HALVES[half]].bitcast(fp32), SUB).then_inc(attn_split, 1)

                def out(c):
                    dve.wait_ge(out_mm, CHUNKS * b + c + 1)
                    if c == 0 and not first:
                        dve.wait_ge(out_stored, 16 * CHUNKS * b)
                    nc.vector.tensor_tensor(outT[:, c, :], out_banks[c][:, :], x2T[:, c, :], ADD).then_inc(out_done, 1)

                def x1(c):
                    dve.wait_ge(wo_mm, CHUNKS * a + c + 1)
                    nc.vector.tensor_tensor(x1T[:, c, :], early[c][:, :], xT[pa][:, c, :], ADD).then_inc(x1_done, 1)

                if has_early:
                    for i in range(4):
                        maxima(i)
                if has_late:
                    split_h(0)
                if has_early:
                    for i in range(4, HEADS):
                        maxima(i)
                if has_late:
                    split_h(1)
                    split_h(2)
                    split_h(3)
                if has_early and has_next:
                    round_x()
                if has_late:
                    x2(0)
                    round_keys()
                    x2(1)
                else:
                    split_wo()
                    split_w1()
                if has_early:
                    merge_heads()
                    invert(0)
                if has_late:
                    x2(2)
                if has_early:
                    invert(1)
                    swap_inverses(0)
                    divide(0)
                    swap_inverses(1)
                    divide(1)
                if has_late:
                    x2(3)
                if has_early:
                    split_attn(0)
                    split_attn(1)
                if has_late:
                    late_maxima()
                if has_early:
                    x1(0)
                    x1(1)
                if has_late:
                    late_normalise()
                if has_early:
                    x1(2)
                    x1(3)
                if has_late:
                    split_late_probsT()
                if has_early and has_next:
                    split_k(a + 1)
                if has_late:
                    for c in range(CHUNKS):
                        out(c)
                if has_early and has_next:
                    split_q(a + 1)

            run_steps(dve, step)

        @block.tensor
        def _(pe):
            def three_passes(out, pairs, first=True, last=True):
                for n, ((w_hi, w_lo), (m_hi, m_lo)) in enumerate(pairs):
                    nc.tensor.matmul(out, w_hi, m_hi, start=first and n == 0, stop=False)
                    nc.tensor.matmul(out, w_hi, m_lo, start=False, stop=False)
                    result = nc.tensor.matmul(out, w_lo, m_hi, start=False, stop=last and n == len(pairs) - 1)
                return result

            def project_q(n, chunks, first_batch=False):
                if not first_batch and 0 in chunks:
                    pe.wait_ge(x_split, n)
                    pe.wait_ge(numer_done, n)
                for c in chunks:
                    if first_batch:
                        pe.wait_ge(first_x_split, c + 1)
                    last = three_passes(odds[:, :], [((wq_hi[:, c, :], wq_lo[:, c, :]), (xT_hi[:, c, :], xT_lo[:, c, :]))],
                                        first=c == 0, last=c == CHUNKS - 1)
                if CHUNKS - 1 in chunks:
                    last.then_inc(q_mm, 1)

            def project_k(n, first_batch=False):
                pe.wait_ge(early_keysT_loaded, 16 * (n + 1))
                if not first_batch:
                    pe.wait_ge(even_numer_done, n)
                for c in range(CHUNKS):
                    last = nc.tensor.matmul(evens[:, 0:KEYS], wk[:, c, :], early_keysT[:, c, :], start=c == 0, stop=c == CHUNKS - 1)
                last.then_inc(k_mm, 1)

            def project_v(n, first_batch=False):
                if not first_batch:
                    pe.wait_ge(x1_done, CHUNKS * (n - 1) + 1)
                for c in range(CHUNKS):
                    last = nc.tensor.matmul(early[0][0:KEYS, 0:PROJ], early_keysT[:, c, :], wv[:, c, :],
                                            start=c == 0, stop=c == CHUNKS - 1)
                last.then_inc(v_mm, 1)

            pe.wait_ge(kv_weights_loaded, 32)
            project_k(0, first_batch=True)
            project_v(0, first_batch=True)
            pe.wait_ge(wq_split, 2)
            project_q(0, range(CHUNKS), first_batch=True)

            def step(pair, p, has_late=True, has_early=True, first=False, has_next=True):
                b = 2 * pair + p
                a = b + 1

                def rank(i):
                    t, half = i % TILES, i // TILES
                    if i == 0:
                        pe.wait_ge(k_built, 2 * a + 2)
                        pe.wait_ge(v_copied, a + 1)
                    if t == 0:
                        pe.wait_ge(q_stacked, 2 * a + half + 1)
                        pe.wait_ge(q_split, PAIRS * a + 2 * half + 2)
                    if i == 1 and has_late:
                        pe.wait_ge(x1_done, CHUNKS * a)
                    if i == 2 and has_late and not first:
                        pe.wait_ge(out_done, CHUNKS * b)
                    if i >= 4:
                        pe.wait_ge(max_done, HEADS * a + i - 3)
                    for n in range(2):
                        pair_ = 2 * half + n
                        last = nc.tensor.matmul(early[i % 4][:, 2 * KEYS * n:2 * KEYS * (n + 1)], q_stack[0:STACK, pair_, t * PART:(t + 1) * PART],
                                                k_stack[0:STACK, 2 * pair_:2 * pair_ + 2, :], start=True, stop=True)
                    last.then_inc(rank_mm, 1)

                def transpose_maxima():
                    if not has_late:
                        pe.wait_ge(small_loaded, 16 * 4)
                    pe.wait_ge(max_done, HEADS * (a + 1))
                    for t in range(TILES):
                        last = nc.tensor.transpose(evens[0:STACK_MAX, t * PART:(t + 1) * PART], neg_max[:, t, :], ident[:, :])
                    last.then_inc(maxT_mm, 1)

                def score(i):
                    h = HEAD_ORDER[i]
                    if i < 4:
                        pe.wait_ge(max_stacked, 2 * a + 1 + i // 2)
                    else:
                        pe.wait_ge(exp_done, HEADS * a + i - 3)
                    nc.tensor.matmul(early[i % 4][0:KEYS, :], k_stack[0:STACK_MAX, h, :], q_stack[0:STACK_MAX, h // 2, :],
                                     start=True, stop=True).then_inc(score_mm, 1)

                def weigh_values(odd):
                    for j in range(PAIRS):
                        pe.wait_ge(exp_done, HEADS * a + HALF * odd + j + 1)
                        h, tile = 2 * j + odd, slice(PAIR_ROWS * j, PAIR_ROWS * (j + 1))
                        last = nc.tensor.matmul((odds if odd else evens)[tile, :], v_ones[:, h, :], probs[:, h, :],
                                                start=True, stop=True, tile_position=(0, PAIR_ROWS * j))
                    last.then_inc(pv_mm, 1)

                def project_out(c):
                    if c == 0:
                        pe.wait_ge(attn_split, 2 * a + 2)
                        if not has_late:
                            pe.wait_ge(wo_split, 2)
                    cols = slice(c * PART, (c + 1) * PART)
                    three_passes(early[c][:, :], [((wo_hi[:, cols], wo_lo[:, cols]), (attnT_hi[:, :], attnT_lo[:, :]))]).then_inc(wo_mm, 1)

                def up(f):
                    if first and f == 0:
                        pe.wait_ge(w1_split, 2)
                    if f < 2 and not first:
                        pe.wait_ge(out_done, CHUNKS * (b - 1) + f + 1)
                    if f >= 2:
                        pe.wait_ge(h_rounded, CHUNKS * b + f - 1)
                    cols = slice(f * PART, (f + 1) * PART)
                    for c in range(CHUNKS):
                        if f == 0:
                            pe.wait_ge(x1_split, CHUNKS * b + c + 1)
                        result = three_passes(late[f % 2][:, :], [((w1T_hi[:, c, cols], w1T_lo[:, c, cols]), (x1T_hi[:, c, :], x1T_lo[:, c, :]))],
                                              first=c == 0, last=c == CHUNKS - 1)
                    result.then_inc(up_mm, 1)

                def down(d):
                    if first and d == 0:
                        pe.wait_ge(w2_split, 2)
                    if d == 1:
                        pe.wait_ge(h_rounded, CHUNKS * (b + 1))
                    if d >= 2:
                        pe.wait_ge(x2_done, CHUNKS * b + d - 1)
                    cols = slice(d * PART, (d + 1) * PART)
                    for c in range(CHUNKS):
                        if d == 0:
                            pe.wait_ge(h_split, CHUNKS * b + max(c, 2) + 1)
                        result = three_passes(late[d % 2][:, :], [((w2T_hi[:, c, cols], w2T_lo[:, c, cols]), (hT_hi[:, c, :], hT_lo[:, c, :]))],
                                              first=c == 0, last=c == CHUNKS - 1)
                    result.then_inc(down_mm, 1)

                def late_scores(chunks):
                    if 0 in chunks:
                        pe.wait_ge(late_keysT_loaded, 16 * (b + 1))
                    for c in chunks:
                        pe.wait_ge(x2_done, CHUNKS * b + max(c, 2) + 1)
                        for t in range(TILES):
                            last = nc.tensor.matmul(late[0][:, t * KEYS:(t + 1) * KEYS], x2T[:, c, t * PART:(t + 1) * PART],
                                                    late_keysT[:, c, :], start=c == 0 and t == 0, stop=c == CHUNKS - 1,
                                                    skip_group_check=True)
                    if CHUNKS - 1 in chunks:
                        last.then_inc(late_score_mm, 1)

                def late_transpose():
                    pe.wait_ge(late_norm_done, b + 1)
                    for t in range(TILES):
                        last = nc.tensor.transpose(late[1][0:KEYS, t * PART:(t + 1) * PART], late_norm[:, t, :], ident[:, :])
                    last.then_inc(late_T_mm, 1)

                def output(c):
                    if c == 0:
                        pe.wait_ge(late_T_split, b + 1)
                        pe.wait_ge(keys_split, b + 1)
                    if c >= 2 and has_early:
                        pe.wait_ge(x1_done, CHUNKS * a + c + 1)
                    cols = slice(c * PART, (c + 1) * PART)
                    three_passes(out_banks[c][:, :], [((keys_hi[:, cols], keys_lo[:, cols]), (late_probsT_hi[:, :], late_probsT_lo[:, :]))]).then_inc(out_mm, 1)

                if has_late:
                    up(0)
                if has_early:
                    for i in range(4):
                        rank(i)
                if has_late:
                    up(1)
                if has_early:
                    for i in range(4, HEADS):
                        rank(i)
                if has_late:
                    up(2)
                if has_early:
                    transpose_maxima()
                if has_late:
                    up(3)
                if has_early:
                    for i in range(4):
                        score(i)
                if has_late:
                    down(0)
                if has_early:
                    for i in range(4, HEADS):
                        score(i)
                if has_late:
                    down(1)
                if has_early:
                    weigh_values(0)
                    weigh_values(1)
                if has_late:
                    down(2)
                    down(3)
                    late_scores(range(3))
                q_first, q_rest = (range(1), range(1, CHUNKS)) if has_late else (range(CHUNKS), [])
                if has_early and has_next:
                    project_q(a + 1, q_first)
                if has_late:
                    late_scores(range(3, CHUNKS))
                if has_early:
                    for c in range(CHUNKS):
                        project_out(c)
                if has_early and has_next:
                    project_k(a + 1)
                if has_late:
                    late_transpose()
                if has_early and has_next:
                    project_q(a + 1, q_rest)
                    project_v(a + 1)
                if has_late:
                    for c in range(CHUNKS):
                        output(c)

            run_steps(pe, step)


def kernel(x, ctx_1024, L0_xattn_W_q, L0_xattn_W_k, L0_xattn_W_v, L0_xattn_W_o,
           L0_xattn_w1, L0_xattn_b1, L0_xattn_w2, L0_xattn_b2):
    import numpy as np
    import concourse.bacc as bacc
    from concourse.bass_utils import run_bass_kernel_spmd

    def by_partition(w):
        w = np.asarray(w)
        return w.reshape(CHUNKS, PART, w.shape[1]).transpose(1, 0, 2)

    x, ctx = np.asarray(x), np.asarray(ctx_1024)
    row, head = np.arange(PART)[:, None], np.arange(HEADS)[None, :]
    inputs = {
        "xT": x.reshape(BATCHES, QUERIES, CHUNKS, PART).transpose(0, 3, 2, 1),
        "ctx": ctx,
        "ctxT": ctx.reshape(BATCHES, KEYS, CHUNKS, PART).transpose(0, 3, 2, 1),
        "wq": by_partition(L0_xattn_W_q),
        "wk": by_partition(L0_xattn_W_k),
        "wv": by_partition(L0_xattn_W_v),
        "wo": np.asarray(L0_xattn_W_o),
        "w1T": by_partition(np.asarray(L0_xattn_w1).T),
        "b1": np.asarray(L0_xattn_b1).reshape(CHUNKS, PART).T,
        "w2T": by_partition(np.asarray(L0_xattn_w2).T),
        "b2": np.asarray(L0_xattn_b2).reshape(CHUNKS, PART).T,
        "ident": np.eye(PART, dtype=np.float32),
        "pair_rows": (row // HEAD_DIM % 2 == head[:, :2]).astype(np.float32),
        "max_rows": (row == STACK + head).astype(np.float32),
    }
    inputs = {name + "_dram": np.ascontiguousarray(a) for name, a in inputs.items()}
    nc = bacc.Bacc("TRN2", target_bir_lowering=False, num_devices=1)
    args = [nc.dram_tensor(name, a.shape, mybir.dt.from_np(a.dtype), kind="ExternalInput").ap()
            for name, a in inputs.items()]
    outT = nc.dram_tensor("outT_dram", (BATCHES, PART, CHUNKS, QUERIES), mybir.dt.float32, kind="ExternalOutput").ap()
    cross_attention_ffn_attention(nc, *args, outT)
    result = run_bass_kernel_spmd(nc, [inputs], core_ids=[0]).results[0]["outT_dram"]
    return np.ascontiguousarray(result.transpose(0, 3, 2, 1)).reshape(BATCHES, QUERIES, DIM)
```

```python
import concourse.bass as bass
from concourse import mybir
from concourse.alu_op_type import AluOpType
from contextlib import ExitStack

BATCHES, QUERIES, DIM, KEYS = 16, 512, 512, 120
HEADS, HEAD_DIM = 8, 16
PART = 128
CHUNKS = DIM // PART
TILES = QUERIES // PART
PROJ = HEADS * HEAD_DIM
HALF = HEADS // 2
SCALE = HEAD_DIM ** -0.5
PAIRS = HEADS // 2
PAIR_ROWS = 2 * HEAD_DIM
STACK = 3 * PAIR_ROWS
STACK_MAX = STACK + HEADS
HEAD_ORDER = [0, 2, 4, 6, 1, 3, 5, 7]
SWAP_HEADS = [(r + HEAD_DIM) % PAIR_ROWS for r in range(PAIR_ROWS)]
HALVES = [slice(0, QUERIES // 2), slice(QUERIES // 2, QUERIES)]
QUERIES_OF = {None: slice(0, QUERIES), 0: HALVES[0], 1: HALVES[1]}
TILES_OF = {None: range(TILES), 0: range(TILES // 2), 1: range(TILES // 2, TILES)}
CHUNK_PAIRS = [slice(0, 2), slice(2, 4)]


def cross_attention_ffn_attention(nc, xT_d, ctx_d, ctxT_d, wq_d, wk_d, wv_d, wo_d, w1T_d, b1_d, w2T_d, b2_d,
                                  ident_d, pair_rows_d, max_rows_d, outT_d):
    fp32, fp32r = mybir.dt.float32, mybir.dt.float32r
    ACT, AX = mybir.ActivationFunctionType, mybir.AxisListType
    ADD, SUB, MULT = AluOpType.add, AluOpType.subtract, AluOpType.mult

    with ExitStack() as ctx:
        def sb(name, shape, dt=fp32):
            return ctx.enter_context(nc.sbuf_tensor(name, shape, dt))

        def bank(name):
            return ctx.enter_context(nc.psum_tensor(name, [PART, 512], fp32))

        def sem(name):
            return ctx.enter_context(nc.semaphore(name))

        def split(name, shape):
            return sb(name + "_hi", shape, fp32r), sb(name + "_lo", shape, fp32r)

        wk = sb("wk", [PART, CHUNKS, PROJ])
        wv = sb("wv", [PART, CHUNKS, PROJ])
        wq = sb("wq", [PART, CHUNKS, PROJ])
        wo = sb("wo", [PROJ, DIM])
        wq_hi, wq_lo = split("wq", [PART, CHUNKS, PROJ])
        wo_hi, wo_lo = split("wo", [PROJ, DIM])
        w1T_hi, w1T_lo = split("w1T", [PART, CHUNKS, DIM])
        w2T_hi, w2T_lo = split("w2T", [PART, CHUNKS, DIM])
        b1 = sb("b1", [PART, CHUNKS])
        b2 = sb("b2", [PART, CHUNKS])
        ident = sb("ident", [PART, PART])
        pair_rows = sb("pair_rows", [PART, 2])
        max_rows = sb("max_rows", [PART, HEADS])

        xT = [sb(f"xT{p}", [PART, CHUNKS, QUERIES]) for p in range(2)]
        early_keysT = sb("early_keysT", [PART, CHUNKS, KEYS])
        late_keysT = sb("late_keysT", [PART, CHUNKS, KEYS])
        keys = [sb(f"keys{p}", [KEYS, DIM]) for p in range(2)]
        xT_hi, xT_lo = split("xT", [PART, CHUNKS, QUERIES])
        keys_hi, keys_lo = split("keys", [KEYS, DIM])

        k_parts = sb("k_parts", [STACK, PAIRS, KEYS], fp32r)
        k_stack = sb("k_stack", [PART, HEADS, KEYS], fp32r)
        v_ones = sb("v_ones", [KEYS, HEADS, PAIR_ROWS])
        q_stack = sb("q_stack", [PART, PAIRS, QUERIES], fp32r)
        neg_max = sb("neg_max", [PART, TILES, STACK_MAX])
        probs = sb("probs", [KEYS, HEADS, QUERIES])
        even_numer = sb("even_numer", [PROJ, QUERIES])
        even_sum = sb("even_sum", [PROJ, QUERIES])
        swapped_sum = sb("swapped_sum", [PROJ, QUERIES])
        inv_sum = sb("inv_sum", [PROJ, QUERIES])
        attnT = sb("attnT", [PROJ, QUERIES])
        attnT_hi, attnT_lo = split("attnT", [PROJ, QUERIES])
        x1T = sb("x1T", [PART, CHUNKS, QUERIES])
        x1T_hi, x1T_lo = split("x1T", [PART, CHUNKS, QUERIES])

        hT = sb("hT", [PART, 2, QUERIES])
        hT_hi, hT_lo = split("hT", [PART, CHUNKS, QUERIES])
        x2T = sb("x2T", [PART, CHUNKS, QUERIES])
        late_neg_max = sb("late_neg_max", [PART, TILES])
        late_probs = sb("late_probs", [PART, TILES, KEYS])
        late_sum = sb("late_sum", [PART, TILES])
        late_inv = sb("late_inv", [PART, TILES])
        late_norm = sb("late_norm", [PART, TILES, KEYS])
        late_probsT_hi, late_probsT_lo = split("late_probsT", [KEYS, QUERIES])
        outT = sb("outT", [PART, CHUNKS, QUERIES])
        w1T, w2T = x2T, outT

        late = [bank(f"late{i}") for i in range(2)]
        early = [bank(f"early{i}") for i in range(4)]
        evens = bank("evens")
        odds = bank("odds")

        out_banks = [late[0], late[1], early[2], early[3]]
        half_banks = [[late[0], early[0], early[1], early[2]], [early[3], evens, odds, late[1]]]

        masks_loaded = sem("masks_loaded")
        kv_weights_loaded = sem("kv_weights_loaded")
        wq_loaded = sem("wq_loaded")
        small_loaded = sem("small_loaded")
        ffn_loaded = sem("ffn_loaded")
        first_x_loaded = [sem(f"first_x_loaded{c}") for c in range(CHUNKS)]
        x_loaded = [sem(f"x_loaded{p}") for p in range(2)]
        early_keysT_loaded = sem("early_keysT_loaded")
        late_keysT_loaded = sem("late_keysT_loaded")
        keys_loaded = [sem(f"keys_loaded{p}") for p in range(2)]
        out_stored = sem("out_stored")
        ones_set = sem("ones_set")
        max_rows_set = sem("max_rows_set")
        neg_max_cleared = sem("neg_max_cleared")
        wq_split = sem("wq_split")
        wo_split = sem("wo_split")
        w1_split = sem("w1_split")
        w2_split = sem("w2_split")
        first_x_rounded = sem("first_x_rounded")
        x_rounded = sem("x_rounded")
        first_x_split = sem("first_x_split")
        x_split = sem("x_split")
        k_mm = sem("k_mm")
        v_mm = sem("v_mm")
        k_rounded = sem("k_rounded")
        k_split = sem("k_split")
        v_copied = sem("v_copied")
        k_built = sem("k_built")
        q_mm = sem("q_mm")
        q_rounded = sem("q_rounded")
        q_split = sem("q_split")
        q_stacked = sem("q_stacked")
        rank_mm = sem("rank_mm")
        max_done = sem("max_done")
        maxT_mm = sem("maxT_mm")
        max_stacked = sem("max_stacked")
        score_mm = sem("score_mm")
        exp_done = sem("exp_done")
        pv_mm = sem("pv_mm")
        even_sum_done = sem("even_sum_done")
        even_numer_done = sem("even_numer_done")
        sum_swapped = sem("sum_swapped")
        numer_done = sem("numer_done")
        inv_swapped = sem("inv_swapped")
        inv_done = sem("inv_done")
        attn_done = sem("attn_done")
        attn_rounded = sem("attn_rounded")
        attn_split = sem("attn_split")
        wo_mm = sem("wo_mm")
        x1_done = sem("x1_done")
        x1_rounded = sem("x1_rounded")
        x1_split = sem("x1_split")
        up_mm = sem("up_mm")
        h_rounded = sem("h_rounded")
        h_split = sem("h_split")
        down_mm = sem("down_mm")
        x2_done = sem("x2_done")
        late_score_mm = sem("late_score_mm")
        late_max_done = sem("late_max_done")
        late_exp_done = sem("late_exp_done")
        late_inv_done = sem("late_inv_done")
        late_norm_done = sem("late_norm_done")
        late_T_mm = sem("late_T_mm")
        late_T_rounded = sem("late_T_rounded")
        late_T_split = sem("late_T_split")
        keys_rounded = sem("keys_rounded")
        keys_split = sem("keys_split")
        out_mm = sem("out_mm")
        out_done = sem("out_done")

        block = ctx.enter_context(nc.Block())

        def run_steps(engine, step):
            step(-1, 1, has_late=False)
            step(0, 0, first=True)
            with engine.Fori(0, BATCHES // 2 - 2) as pair:
                step(pair, 1)
                step(pair + 1, 0)
            step(BATCHES // 2 - 2, 1)
            step(BATCHES // 2 - 1, 0, has_next=False)
            step(BATCHES // 2 - 1, 1, has_early=False)

        @block.sync
        def _(sp):
            def load_x(b, p):
                sp.dma_start(xT[p][:, :, :], xT_d[bass.ds(b, 1)].rearrange("o p c q -> p (o c) q")).then_inc(x_loaded[p], 16)

            def load_early_keysT(b):
                sp.dma_start(early_keysT[:, :, :], ctxT_d[bass.ds(b, 1)].rearrange("o p c k -> p (o c) k")).then_inc(early_keysT_loaded, 16)

            def load_late_keysT(b):
                sp.dma_start(late_keysT[:, :, :], ctxT_d[bass.ds(b, 1)].rearrange("o p c k -> p (o c) k")).then_inc(late_keysT_loaded, 16)

            def load_keys(b, p):
                sp.dma_start(keys[p][:, :], ctx_d[bass.ds(b, 1)].rearrange("o k d -> k (o d)")).then_inc(keys_loaded[p], 16)

            sp.dma_start(wk[:, :, :], wk_d).then_inc(kv_weights_loaded, 16)
            load_early_keysT(0)
            sp.dma_start(wv[:, :, :], wv_d).then_inc(kv_weights_loaded, 16)
            sp.dma_start(wq[:, :, :], wq_d).then_inc(wq_loaded, 16)
            for c in range(CHUNKS):
                sp.dma_start(xT[0][:, c, :], xT_d[0, :, c, :]).then_inc(first_x_loaded[c], 16)
            sp.dma_start(pair_rows[:, :], pair_rows_d).then_inc(masks_loaded, 16)
            sp.dma_start(max_rows[:, :], max_rows_d).then_inc(masks_loaded, 16)
            sp.dma_start(ident[:, :], ident_d).then_inc(small_loaded, 16)
            sp.dma_start(wo[:, :], wo_d).then_inc(small_loaded, 16)
            sp.dma_start(b1[:, :], b1_d).then_inc(small_loaded, 16)
            sp.dma_start(b2[:, :], b2_d).then_inc(small_loaded, 16)
            load_x(1, 1)
            sp.dma_start(w1T[:, :, :], w1T_d).then_inc(ffn_loaded, 16)
            sp.wait_ge(v_mm, 1)
            load_early_keysT(1)
            load_late_keysT(0)
            sp.dma_start(w2T[:, :, :], w2T_d).then_inc(ffn_loaded, 16)
            load_keys(0, 0)
            load_keys(1, 1)

            def step(pair, p, loads=True, last=False):
                b = 2 * pair + p
                if loads:
                    sp.wait_ge(v_mm, b + 2)
                    load_early_keysT(b + 2)
                    sp.wait_ge(x1_done, CHUNKS * b + CHUNKS)
                    load_x(b + 2, p)
                if not last:
                    sp.wait_ge(late_score_mm, b + 1)
                    load_late_keysT(b + 1)
                    for c in range(CHUNKS):
                        sp.wait_ge(out_done, CHUNKS * b + c + 1)
                        sp.dma_start(outT_d[bass.ds(b, 1), :, c, :].rearrange("o p q -> p (o q)"), outT[:, c, :]).then_inc(out_stored, 16)
                else:
                    for n in range(4):
                        half, chunks = n // 2, CHUNK_PAIRS[n % 2]
                        sp.wait_ge(out_done, CHUNKS * b + n + 1)
                        sp.dma_start(outT_d[b, :, chunks, HALVES[half]], outT[:, chunks, HALVES[half]]).then_inc(out_stored, 16)
                if loads:
                    load_keys(b + 2, p)

            step(0, 0)
            with sp.Fori(0, BATCHES // 2 - 2) as pair:
                step(pair, 1)
                step(pair + 1, 0)
            step(BATCHES // 2 - 2, 1)
            step(BATCHES // 2 - 1, 0, loads=False)
            step(BATCHES // 2 - 1, 1, loads=False, last=True)
            sp.wait_ge(out_stored, 16 * CHUNKS * BATCHES)

        @block.gpsimd
        def _(pool):
            nc.gpsimd.memset(v_ones[:, :, :], 1.0).then_inc(ones_set, 1)
            pool.wait_ge(masks_loaded, 32)
            nc.gpsimd.tensor_copy(k_stack[:, :, :], max_rows[:, :].unsqueeze(2).to_broadcast([PART, HEADS, KEYS])).then_inc(max_rows_set, 1)
            pool.wait_ge(max_rows_set, 1)

            def build_k(n):
                pool.wait_ge(k_split, n + 1)
                stack = k_stack[0:STACK, :, :].rearrange("r (pair odd) k -> r pair odd k", odd=2)
                for odd in range(2):
                    rows = pair_rows[0:STACK, odd:odd + 1].unsqueeze(2).to_broadcast([STACK, PAIRS, KEYS])
                    nc.gpsimd.tensor_tensor(stack[:, :, odd, :], k_parts[:, :, :].bitcast(fp32), rows, MULT).then_inc(k_built, 1)
                    pool.wait_ge(k_built, 2 * n + odd + 1)

            build_k(0)

            def split_x(n, p):
                pool.wait_ge(x_rounded, n)
                nc.gpsimd.tensor_tensor(xT_lo[:, :, :], xT[p][:, :, :], xT_hi[:, :, :].bitcast(fp32), SUB).then_inc(x_split, 1)
                pool.wait_ge(x_split, n)

            def step(pair, p, has_late=True, has_early=True, first=False, has_next=True):
                b = 2 * pair + p
                a = b + 1
                if has_early and has_next:
                    split_x(a + 1, p)
                if not has_late:
                    pool.wait_ge(ffn_loaded, 32)
                    nc.gpsimd.tensor_copy(w2T_hi[:, :, :], w2T[:, :, :]).then_inc(w2_split, 1)
                    pool.wait_ge(w2_split, 1)
                    nc.gpsimd.tensor_tensor(w2T_lo[:, :, :], w2T[:, :, :], w2T_hi[:, :, :].bitcast(fp32), SUB).then_inc(w2_split, 1)
                    pool.wait_ge(w2_split, 2)
                if has_late:
                    pool.wait_ge(keys_rounded, b + 1)
                    nc.gpsimd.tensor_tensor(keys_lo[:, :], keys[p][:, :], keys_hi[:, :].bitcast(fp32), SUB).then_inc(keys_split, 1)
                    pool.wait_ge(keys_split, b + 1)
                if has_early:
                    for c in range(CHUNKS):
                        pool.wait_ge(x1_rounded, CHUNKS * a + c + 1)
                        nc.gpsimd.tensor_tensor(x1T_lo[:, c, :], x1T[:, c, :], x1T_hi[:, c, :].bitcast(fp32), SUB).then_inc(x1_split, 1)
                    pool.wait_ge(x1_split, CHUNKS * (a + 1))
                if has_early and has_next:
                    build_k(a + 1)

            run_steps(pool, step)

        @block.scalar
        def _(act):
            def round_k(n):
                act.wait_ge(k_mm, n + 1)
                for pair_ in range(PAIRS):
                    last = nc.scalar.copy(k_parts[0:PAIR_ROWS, pair_, :], evens[PAIR_ROWS * pair_:PAIR_ROWS * (pair_ + 1), 0:KEYS])
                last.then_inc(k_rounded, 1)

            def copy_v(n, first_batch=False):
                act.wait_ge(v_mm, n + 1)
                if not first_batch:
                    act.wait_ge(pv_mm, 2 * n)
                halves = early[0][0:KEYS, 0:PROJ].rearrange("k (pair odd d) -> k pair odd d", odd=2, d=HEAD_DIM)
                pairs = v_ones[:, :, :].rearrange("k (pair odd) c -> k pair odd c", odd=2)
                nc.scalar.copy(pairs[:, :, 0, 0:HEAD_DIM], halves[:, :, 0, :])
                nc.scalar.copy(pairs[:, :, 1, HEAD_DIM:2 * HEAD_DIM], halves[:, :, 1, :]).then_inc(v_copied, 1)

            def stack_q(n):
                act.wait_ge(q_mm, n + 1)
                for half in range(2):
                    for pair_ in range(2 * half, 2 * half + 2):
                        nc.scalar.copy(q_stack[0:PAIR_ROWS, pair_, :], odds[PAIR_ROWS * pair_:PAIR_ROWS * (pair_ + 1), :]).then_inc(q_rounded, 1)
                    act.wait_ge(q_rounded, PAIRS * n + 2 * half + 2)
                    nc.scalar.copy(q_stack[2 * PAIR_ROWS:STACK, 2 * half:2 * half + 2, :],
                                   q_stack[0:PAIR_ROWS, 2 * half:2 * half + 2, :].bitcast(fp32)).then_inc(q_stacked, 1)

            act.wait_ge(wq_loaded, 16)
            nc.scalar.copy(wq_hi[:, :, :], wq[:, :, :]).then_inc(wq_split, 1)
            for c in range(CHUNKS):
                act.wait_ge(first_x_loaded[c], 16)
                nc.scalar.copy(xT_hi[:, c, :], xT[0][:, c, :]).then_inc(first_x_rounded, 1)
            act.wait_ge(ones_set, 1)
            act.wait_ge(masks_loaded, 32)
            round_k(0)
            copy_v(0, first_batch=True)
            stack_q(0)

            def step(pair, p, has_late=True, has_early=True, first=False, has_next=True):
                b = 2 * pair + p
                a = b + 1

                def relu(c):
                    act.wait_ge(up_mm, CHUNKS * b + c + 1)
                    if first and c == 0:
                        act.wait_ge(small_loaded, 16 * 4)
                    if c >= 2 or not first:
                        act.wait_ge(h_split, CHUNKS * b + c - 1)
                    nc.scalar.activation(hT[:, c % 2, :], late[c % 2][:, :], ACT.Relu, bias=b1[:, c:c + 1])
                    nc.scalar.activation(hT_hi[:, c, :], late[c % 2][:, :], ACT.Relu, bias=b1[:, c:c + 1]).then_inc(h_rounded, 1)

                def stack_maxima():
                    act.wait_ge(maxT_mm, a + 1)
                    for half in range(2):
                        nc.scalar.copy(q_stack[STACK:STACK_MAX, 2 * half:2 * half + 2, :],
                                       evens[STACK:STACK_MAX, :].unsqueeze(1).to_broadcast([HEADS, 2, QUERIES])).then_inc(max_stacked, 1)

                def exp(i):
                    act.wait_ge(score_mm, HEADS * a + i + 1)
                    nc.scalar.activation(probs[:, HEAD_ORDER[i], :], early[i % 4][0:KEYS, :], ACT.Exp, scale=SCALE).then_inc(exp_done, 1)

                def late_exps(half=None):
                    bank = late[0] if half is None else half_banks[half][0]
                    act.wait_ge(late_max_done, b + 1 + (half or 0))
                    for n, t in enumerate(TILES_OF[half]):
                        nc.scalar.activation(late_probs[:, t, :], bank[:, n * KEYS:(n + 1) * KEYS], ACT.Exp,
                                             bias=late_neg_max[:, t:t + 1], accum_out=late_sum[:, t:t + 1]).then_inc(late_exp_done, 1)

                def round_late_probsT(half=None):
                    bank = late[1] if half is None else half_banks[half][1]
                    width = len(TILES_OF[half]) * PART
                    act.wait_ge(late_T_mm, b + 1 + (half or 0))
                    nc.scalar.copy(late_probsT_hi[:, QUERIES_OF[half]], bank[0:KEYS, 0:width]).then_inc(late_T_rounded, 1)

                def part_evens():
                    act.wait_ge(pv_mm, 2 * a + 1)
                    nc.scalar.activation(even_sum[:, :], evens[:, :], ACT.Identity, scale=pair_rows[:, 1:2]).then_inc(even_sum_done, 1)
                    nc.scalar.activation(even_numer[:, :], evens[:, :], ACT.Identity, scale=pair_rows[:, 0:1]).then_inc(even_numer_done, 1)

                def round_attn(half):
                    act.wait_ge(attn_done, 2 * a + half + 1)
                    nc.scalar.copy(attnT_hi[:, HALVES[half]], attnT[:, HALVES[half]]).then_inc(attn_rounded, 1)

                def round_x1(c):
                    act.wait_ge(x1_done, CHUNKS * a + c + 1)
                    nc.scalar.copy(x1T_hi[:, c, :], x1T[:, c, :]).then_inc(x1_rounded, 1)

                if has_late:
                    for c in range(3):
                        relu(c)
                if has_early:
                    stack_maxima()
                if has_late:
                    relu(3)
                if has_early:
                    for i in range(HEADS):
                        exp(i)
                    part_evens()
                    round_attn(0)
                    round_attn(1)
                if not has_early:
                    for half in range(2):
                        late_exps(half)
                        round_late_probsT(half)
                    return
                if has_late:
                    late_exps()
                round_x1(0)
                round_x1(1)
                if has_late:
                    round_late_probsT()
                round_x1(2)
                round_x1(3)
                if has_next:
                    round_k(a + 1)
                    copy_v(a + 1)
                    stack_q(a + 1)

            run_steps(act, step)

        @block.vector
        def _(dve):
            nc.vector.memset(neg_max[:, :, :], 0.0).then_inc(neg_max_cleared, 1)
            dve.wait_ge(neg_max_cleared, 1)
            dve.wait_ge(wq_split, 1)
            nc.vector.tensor_tensor(wq_lo[:, :, :], wq[:, :, :], wq_hi[:, :, :].bitcast(fp32), SUB).then_inc(wq_split, 1)
            for c in range(CHUNKS):
                dve.wait_ge(first_x_rounded, c + 1)
                nc.vector.tensor_tensor(xT_lo[:, c, :], xT[0][:, c, :], xT_hi[:, c, :].bitcast(fp32), SUB).then_inc(first_x_split, 1)

            def split_wo():
                dve.wait_ge(small_loaded, 16 * 4)
                nc.vector.tensor_copy(wo_hi[:, :], wo[:, :]).then_inc(wo_split, 1)
                dve.wait_ge(wo_split, 1)
                nc.vector.tensor_tensor(wo_lo[:, :], wo[:, :], wo_hi[:, :].bitcast(fp32), SUB).then_inc(wo_split, 1)

            def split_k(n):
                dve.wait_ge(k_rounded, n + 1)
                for pair_ in range(PAIRS):
                    nc.vector.tensor_tensor(k_parts[2 * PAIR_ROWS:STACK, pair_, :], evens[PAIR_ROWS * pair_:PAIR_ROWS * (pair_ + 1), 0:KEYS],
                                            k_parts[0:PAIR_ROWS, pair_, :].bitcast(fp32), SUB)
                nc.vector.tensor_copy(k_parts[PAIR_ROWS:2 * PAIR_ROWS, :, :].bitcast(fp32),
                                      k_parts[0:PAIR_ROWS, :, :].bitcast(fp32)).then_inc(k_split, 1)

            def split_q(n):
                for pair_ in range(PAIRS):
                    dve.wait_ge(q_rounded, PAIRS * n + pair_ + 1)
                    nc.vector.tensor_tensor(q_stack[PAIR_ROWS:2 * PAIR_ROWS, pair_, :], odds[PAIR_ROWS * pair_:PAIR_ROWS * (pair_ + 1), :],
                                            q_stack[0:PAIR_ROWS, pair_, :].bitcast(fp32), SUB).then_inc(q_split, 1)

            split_k(0)
            split_q(0)

            def step(pair, p, has_late=True, has_early=True, first=False, has_next=True):
                b = 2 * pair + p
                a = b + 1
                pa = 1 - p

                def round_x():
                    dve.wait_ge(x_loaded[p], 16 * (pair + 1 + p))
                    nc.vector.tensor_copy(xT_hi[:, :, :], xT[p][:, :, :]).then_inc(x_rounded, 1)

                def split_w1():
                    dve.wait_ge(ffn_loaded, 32)
                    nc.vector.tensor_copy(w1T_hi[:, :, :], w1T[:, :, :]).then_inc(w1_split, 1)
                    dve.wait_ge(w1_split, 1)
                    nc.vector.tensor_tensor(w1T_lo[:, :, :], w1T[:, :, :], w1T_hi[:, :, :].bitcast(fp32), SUB).then_inc(w1_split, 1)

                def round_keys():
                    dve.wait_ge(keys_loaded[p], 16 * (pair + 1))
                    nc.vector.tensor_copy(keys_hi[:, :], keys[p][:, :]).then_inc(keys_rounded, 1)

                def maxima(i):
                    t, half = i % TILES, i // TILES
                    dve.wait_ge(rank_mm, HEADS * a + i + 1)
                    scores = early[i % 4][:, 0:HALF * KEYS].rearrange("q (h k) -> q h k", k=KEYS)
                    at = STACK + HALF * half
                    nc.vector.reduce_max(neg_max[:, t, at:at + HALF], scores, AX.X, negate=True).then_inc(max_done, 1)

                def split_h(c):
                    dve.wait_ge(h_rounded, CHUNKS * b + c + 1)
                    nc.vector.tensor_tensor(hT_lo[:, c, :], hT[:, c % 2, :], hT_hi[:, c, :].bitcast(fp32), SUB).then_inc(h_split, 1)

                def x2(c, half=None):
                    bank = late[c % 2] if half is None else half_banks[half][c]
                    queries, width = QUERIES_OF[half], len(TILES_OF[half]) * PART
                    dve.wait_ge(down_mm, CHUNKS * b + c + 1 + CHUNKS * (half or 0))
                    nc.vector.scalar_tensor_tensor(x2T[:, c, queries], bank[:, 0:width], b2[:, c:c + 1], x1T[:, c, queries], ADD, ADD).then_inc(x2_done, 1)

                def late_maxima(half=None):
                    bank = late[0] if half is None else half_banks[half][0]
                    tiles = TILES_OF[half]
                    dve.wait_ge(late_score_mm, b + 1 + (half or 0))
                    scores = bank[:, 0:len(tiles) * KEYS].rearrange("q (t k) -> q t k", k=KEYS)
                    nc.vector.reduce_max(late_neg_max[:, tiles.start:tiles.stop], scores, AX.X, negate=True).then_inc(late_max_done, 1)

                def late_normalise(half=None):
                    first_tile, end = TILES_OF[half].start, TILES_OF[half].stop
                    dve.wait_ge(late_exp_done, TILES * b + end)
                    nc.vector.reciprocal(late_inv[:, first_tile:end], late_sum[:, first_tile:end]).then_inc(late_inv_done, 1)
                    dve.wait_ge(late_inv_done, b + 1 + (half or 0))
                    nc.vector.tensor_tensor(late_norm[:, first_tile:end, :], late_probs[:, first_tile:end, :],
                                            late_inv[:, first_tile:end].unsqueeze(2).to_broadcast([PART, end - first_tile, KEYS]), MULT).then_inc(late_norm_done, 1)

                def split_late_probsT(half=None):
                    bank = late[1] if half is None else half_banks[half][1]
                    queries, width = QUERIES_OF[half], len(TILES_OF[half]) * PART
                    dve.wait_ge(late_T_rounded, b + 1 + (half or 0))
                    nc.vector.tensor_tensor(late_probsT_lo[:, queries], bank[0:KEYS, 0:width], late_probsT_hi[:, queries].bitcast(fp32), SUB).then_inc(late_T_split, 1)

                def merge_heads():
                    dve.wait_ge(pv_mm, 2 * a + 2)
                    dve.wait_ge(even_sum_done, a + 1)
                    nc.vector.scalar_tensor_tensor(swapped_sum[:, :], odds[:, :], pair_rows[:, 0:1], even_sum[:, :], MULT, ADD).then_inc(sum_swapped, 1)
                    dve.wait_ge(even_numer_done, a + 1)
                    nc.vector.scalar_tensor_tensor(attnT[:, :], odds[:, :], pair_rows[:, 1:2], even_numer[:, :], MULT, ADD).then_inc(numer_done, 1)

                def invert(half):
                    if half == 0:
                        dve.wait_ge(sum_swapped, a + 1)
                    else:
                        dve.wait_ge(inv_swapped, 2 * a + 1)
                    nc.vector.reciprocal(swapped_sum[:, HALVES[half]], swapped_sum[:, HALVES[half]]).then_inc(inv_swapped, 1)

                def swap_inverses(half):
                    nc.vector.stream_shuffle(inv_sum[:, HALVES[half]], swapped_sum[:, HALVES[half]], SWAP_HEADS).then_inc(inv_done, 1)

                def divide(half):
                    if half == 0:
                        dve.wait_ge(numer_done, a + 1)
                        dve.wait_ge(inv_swapped, 2 * a + 2)
                    dve.wait_ge(inv_done, 2 * a + half + 1)
                    nc.vector.tensor_tensor(attnT[:, HALVES[half]], attnT[:, HALVES[half]], inv_sum[:, HALVES[half]], MULT).then_inc(attn_done, 1)

                def split_attn(half):
                    dve.wait_ge(attn_rounded, 2 * a + half + 1)
                    nc.vector.tensor_tensor(attnT_lo[:, HALVES[half]], attnT[:, HALVES[half]], attnT_hi[:, HALVES[half]].bitcast(fp32), SUB).then_inc(attn_split, 1)

                def out(c):
                    dve.wait_ge(out_mm, CHUNKS * b + c + 1)
                    if c == 0 and not first:
                        dve.wait_ge(out_stored, 16 * CHUNKS * b)
                    nc.vector.tensor_tensor(outT[:, c, :], out_banks[c][:, :], x2T[:, c, :], ADD).then_inc(out_done, 1)

                def half_out(n, half):
                    chunks, queries = CHUNK_PAIRS[n], HALVES[half]
                    dve.wait_ge(out_mm, CHUNKS * b + 2 * half + n + 1)
                    if n == 0 and half == 0:
                        dve.wait_ge(out_stored, 16 * CHUNKS * b)
                    products = half_banks[half][2 + n][:, :].rearrange("p (c q) -> p c q", c=2)
                    nc.vector.tensor_tensor(outT[:, chunks, queries], products, x2T[:, chunks, queries], ADD).then_inc(out_done, 1)

                def x1(c):
                    dve.wait_ge(wo_mm, CHUNKS * a + c + 1)
                    nc.vector.tensor_tensor(x1T[:, c, :], early[c][:, :], xT[pa][:, c, :], ADD).then_inc(x1_done, 1)

                if has_early:
                    for i in range(4):
                        maxima(i)
                if has_late:
                    split_h(0)
                if has_early:
                    for i in range(4, HEADS):
                        maxima(i)
                if has_late:
                    split_h(1)
                    split_h(2)
                    split_h(3)
                if not has_early:
                    round_keys()
                    for c in range(CHUNKS):
                        x2(c, 0)
                    x2(0, 1)
                    late_maxima(0)
                    x2(1, 1)
                    late_normalise(0)
                    x2(2, 1)
                    split_late_probsT(0)
                    x2(3, 1)
                    half_out(0, 0)
                    late_maxima(1)
                    half_out(1, 0)
                    late_normalise(1)
                    split_late_probsT(1)
                    half_out(0, 1)
                    half_out(1, 1)
                    return
                if has_next:
                    round_x()
                if has_late:
                    x2(0)
                    round_keys()
                    x2(1)
                else:
                    split_wo()
                    split_w1()
                merge_heads()
                invert(0)
                if has_late:
                    x2(2)
                invert(1)
                swap_inverses(0)
                divide(0)
                swap_inverses(1)
                divide(1)
                if has_late:
                    x2(3)
                split_attn(0)
                split_attn(1)
                if has_late:
                    late_maxima()
                x1(0)
                x1(1)
                if has_late:
                    late_normalise()
                x1(2)
                x1(3)
                if has_late:
                    split_late_probsT()
                if has_next:
                    split_k(a + 1)
                if has_late:
                    for c in range(CHUNKS):
                        out(c)
                if has_next:
                    split_q(a + 1)

            run_steps(dve, step)

        @block.tensor
        def _(pe):
            def three_passes(out, w_hi, w_lo, m_hi, m_lo, first=True, last=True):
                nc.tensor.matmul(out, w_hi, m_hi, start=first, stop=False)
                nc.tensor.matmul(out, w_hi, m_lo, start=False, stop=False)
                return nc.tensor.matmul(out, w_lo, m_hi, start=False, stop=last)

            def project_q(n, chunks, first_batch=False):
                if not first_batch and 0 in chunks:
                    pe.wait_ge(x_split, n)
                    pe.wait_ge(numer_done, n)
                for c in chunks:
                    if first_batch:
                        pe.wait_ge(first_x_split, c + 1)
                    last = three_passes(odds[:, :], wq_hi[:, c, :], wq_lo[:, c, :], xT_hi[:, c, :], xT_lo[:, c, :],
                                        first=c == 0, last=c == CHUNKS - 1)
                if CHUNKS - 1 in chunks:
                    last.then_inc(q_mm, 1)

            def project_k(n, first_batch=False):
                pe.wait_ge(early_keysT_loaded, 16 * (n + 1))
                if not first_batch:
                    pe.wait_ge(even_numer_done, n)
                for c in range(CHUNKS):
                    last = nc.tensor.matmul(evens[:, 0:KEYS], wk[:, c, :], early_keysT[:, c, :], start=c == 0, stop=c == CHUNKS - 1)
                last.then_inc(k_mm, 1)

            def project_v(n, first_batch=False):
                if not first_batch:
                    pe.wait_ge(x1_done, CHUNKS * (n - 1) + 1)
                for c in range(CHUNKS):
                    last = nc.tensor.matmul(early[0][0:KEYS, 0:PROJ], early_keysT[:, c, :], wv[:, c, :],
                                            start=c == 0, stop=c == CHUNKS - 1)
                last.then_inc(v_mm, 1)

            pe.wait_ge(kv_weights_loaded, 32)
            project_k(0, first_batch=True)
            project_v(0, first_batch=True)
            pe.wait_ge(wq_split, 2)
            project_q(0, range(CHUNKS), first_batch=True)

            def step(pair, p, has_late=True, has_early=True, first=False, has_next=True):
                b = 2 * pair + p
                a = b + 1

                def rank(i):
                    t, half = i % TILES, i // TILES
                    if i == 0:
                        pe.wait_ge(k_built, 2 * a + 2)
                        pe.wait_ge(v_copied, a + 1)
                    if t == 0:
                        pe.wait_ge(q_stacked, 2 * a + half + 1)
                        pe.wait_ge(q_split, PAIRS * a + 2 * half + 2)
                    if i == 1 and has_late:
                        pe.wait_ge(x1_done, CHUNKS * a)
                    if i == 2 and has_late and not first:
                        pe.wait_ge(out_done, CHUNKS * b)
                    if i >= 4:
                        pe.wait_ge(max_done, HEADS * a + i - 3)
                    for n in range(2):
                        pair_ = 2 * half + n
                        last = nc.tensor.matmul(early[i % 4][:, 2 * KEYS * n:2 * KEYS * (n + 1)], q_stack[0:STACK, pair_, t * PART:(t + 1) * PART],
                                                k_stack[0:STACK, 2 * pair_:2 * pair_ + 2, :], start=True, stop=True)
                    last.then_inc(rank_mm, 1)

                def transpose_maxima():
                    if not has_late:
                        pe.wait_ge(small_loaded, 16 * 4)
                    pe.wait_ge(max_done, HEADS * (a + 1))
                    for t in range(TILES):
                        last = nc.tensor.transpose(evens[0:STACK_MAX, t * PART:(t + 1) * PART], neg_max[:, t, :], ident[:, :])
                    last.then_inc(maxT_mm, 1)

                def score(i):
                    h = HEAD_ORDER[i]
                    if i < 4:
                        pe.wait_ge(max_stacked, 2 * a + 1 + i // 2)
                    else:
                        pe.wait_ge(exp_done, HEADS * a + i - 3)
                    nc.tensor.matmul(early[i % 4][0:KEYS, :], k_stack[0:STACK_MAX, h, :], q_stack[0:STACK_MAX, h // 2, :],
                                     start=True, stop=True).then_inc(score_mm, 1)

                def weigh_values(odd):
                    for j in range(PAIRS):
                        pe.wait_ge(exp_done, HEADS * a + HALF * odd + j + 1)
                        h, tile = 2 * j + odd, slice(PAIR_ROWS * j, PAIR_ROWS * (j + 1))
                        last = nc.tensor.matmul((odds if odd else evens)[tile, :], v_ones[:, h, :], probs[:, h, :],
                                                start=True, stop=True, tile_position=(0, PAIR_ROWS * j))
                    last.then_inc(pv_mm, 1)

                def project_out(c):
                    if c == 0:
                        pe.wait_ge(attn_split, 2 * a + 2)
                        if not has_late:
                            pe.wait_ge(wo_split, 2)
                    cols = slice(c * PART, (c + 1) * PART)
                    three_passes(early[c][:, :], wo_hi[:, cols], wo_lo[:, cols], attnT_hi[:, :], attnT_lo[:, :]).then_inc(wo_mm, 1)

                def up(f):
                    if first and f == 0:
                        pe.wait_ge(w1_split, 2)
                    if f < 2 and not first:
                        pe.wait_ge(out_done, CHUNKS * (b - 1) + f + 1)
                    if f >= 2:
                        pe.wait_ge(h_rounded, CHUNKS * b + f - 1)
                    cols = slice(f * PART, (f + 1) * PART)
                    for c in range(CHUNKS):
                        if f == 0:
                            pe.wait_ge(x1_split, CHUNKS * b + c + 1)
                        result = three_passes(late[f % 2][:, :], w1T_hi[:, c, cols], w1T_lo[:, c, cols], x1T_hi[:, c, :], x1T_lo[:, c, :],
                                              first=c == 0, last=c == CHUNKS - 1)
                    result.then_inc(up_mm, 1)

                def down(d, half=None):
                    if first and d == 0:
                        pe.wait_ge(w2_split, 2)
                    if half is None and d == 1:
                        pe.wait_ge(h_rounded, CHUNKS * (b + 1))
                    if half is None and d >= 2:
                        pe.wait_ge(x2_done, CHUNKS * b + d - 1)
                    bank = late[d % 2] if half is None else half_banks[half][d]
                    queries, width = QUERIES_OF[half], len(TILES_OF[half]) * PART
                    cols = slice(d * PART, (d + 1) * PART)
                    for c in range(CHUNKS):
                        if half is None and d == 0:
                            pe.wait_ge(h_split, CHUNKS * b + max(c, 2) + 1)
                        result = three_passes(bank[:, 0:width], w2T_hi[:, c, cols], w2T_lo[:, c, cols], hT_hi[:, c, queries], hT_lo[:, c, queries],
                                              first=c == 0, last=c == CHUNKS - 1)
                    result.then_inc(down_mm, 1)

                def down_first_half():
                    for c in range(CHUNKS):
                        pe.wait_ge(h_split, CHUNKS * b + max(c, 2) + 1)
                        for d in range(CHUNKS):
                            if c == 0 and d == CHUNKS - 1:
                                pe.wait_ge(out_done, CHUNKS * b)
                            cols = slice(d * PART, (d + 1) * PART)
                            result = three_passes(half_banks[0][d][:, HALVES[0]],
                                                  w2T_hi[:, c, cols], w2T_lo[:, c, cols], hT_hi[:, c, HALVES[0]], hT_lo[:, c, HALVES[0]],
                                                  first=c == 0, last=c == CHUNKS - 1)
                            if c == CHUNKS - 1:
                                result.then_inc(down_mm, 1)

                def late_scores(chunks, half=None):
                    bank = late[0] if half is None else half_banks[half][0]
                    if 0 in chunks:
                        pe.wait_ge(late_keysT_loaded, 16 * (b + 1))
                    for c in chunks:
                        if half is None:
                            pe.wait_ge(x2_done, CHUNKS * b + max(c, 2) + 1)
                        else:
                            pe.wait_ge(x2_done, CHUNKS * (b + half) + c + 1)
                        for n, t in enumerate(TILES_OF[half]):
                            last = nc.tensor.matmul(bank[:, n * KEYS:(n + 1) * KEYS], x2T[:, c, t * PART:(t + 1) * PART],
                                                    late_keysT[:, c, :], start=c == 0 and n == 0, stop=c == CHUNKS - 1,
                                                    skip_group_check=True)
                    if CHUNKS - 1 in chunks:
                        last.then_inc(late_score_mm, 1)

                def late_transpose(half=None):
                    bank = late[1] if half is None else half_banks[half][1]
                    pe.wait_ge(late_norm_done, b + 1 + (half or 0))
                    for n, t in enumerate(TILES_OF[half]):
                        last = nc.tensor.transpose(bank[0:KEYS, n * PART:(n + 1) * PART], late_norm[:, t, :], ident[:, :])
                    last.then_inc(late_T_mm, 1)

                def output(c):
                    if c == 0:
                        pe.wait_ge(late_T_split, b + 1)
                        pe.wait_ge(keys_split, b + 1)
                    if c >= 2 and has_early:
                        pe.wait_ge(x1_done, CHUNKS * a + c + 1)
                    cols = slice(c * PART, (c + 1) * PART)
                    three_passes(out_banks[c][:, :], keys_hi[:, cols], keys_lo[:, cols], late_probsT_hi[:, :], late_probsT_lo[:, :]).then_inc(out_mm, 1)

                def half_output(n, half):
                    queries = HALVES[half]
                    if n == 0:
                        pe.wait_ge(late_T_split, b + 1 + half)
                    if n == 0 and half == 0:
                        pe.wait_ge(keys_split, b + 1)
                    for i in range(2):
                        c = 2 * n + i
                        cols = slice(c * PART, (c + 1) * PART)
                        result = three_passes(half_banks[half][2 + n][:, HALVES[i]],
                                              keys_hi[:, cols], keys_lo[:, cols], late_probsT_hi[:, queries], late_probsT_lo[:, queries])
                    result.then_inc(out_mm, 1)

                if has_late:
                    up(0)
                if has_early:
                    for i in range(4):
                        rank(i)
                if has_late:
                    up(1)
                if has_early:
                    for i in range(4, HEADS):
                        rank(i)
                if has_late:
                    up(2)
                if has_early:
                    transpose_maxima()
                if has_late:
                    up(3)
                if not has_early:
                    down_first_half()
                    down(0, 1)
                    late_scores(range(CHUNKS), 0)
                    down(1, 1)
                    down(2, 1)
                    late_transpose(0)
                    down(3, 1)
                    half_output(0, 0)
                    late_scores(range(CHUNKS), 1)
                    half_output(1, 0)
                    late_transpose(1)
                    half_output(0, 1)
                    half_output(1, 1)
                    return
                for i in range(4):
                    score(i)
                if has_late:
                    down(0)
                for i in range(4, HEADS):
                    score(i)
                if has_late:
                    down(1)
                weigh_values(0)
                weigh_values(1)
                if has_late:
                    down(2)
                    down(3)
                    late_scores(range(3))
                q_first, q_rest = (range(1), range(1, CHUNKS)) if has_late else (range(CHUNKS), [])
                if has_next:
                    project_q(a + 1, q_first)
                if has_late:
                    late_scores(range(3, CHUNKS))
                for c in range(CHUNKS):
                    project_out(c)
                if has_next:
                    project_k(a + 1)
                if has_late:
                    late_transpose()
                if has_next:
                    project_q(a + 1, q_rest)
                    project_v(a + 1)
                if has_late:
                    for c in range(CHUNKS):
                        output(c)

            run_steps(pe, step)


def kernel(x, ctx_1024, L0_xattn_W_q, L0_xattn_W_k, L0_xattn_W_v, L0_xattn_W_o,
           L0_xattn_w1, L0_xattn_b1, L0_xattn_w2, L0_xattn_b2):
    import numpy as np
    import concourse.bacc as bacc
    from concourse.bass_utils import run_bass_kernel_spmd

    def by_partition(w):
        w = np.asarray(w)
        return w.reshape(CHUNKS, PART, w.shape[1]).transpose(1, 0, 2)

    x, ctx = np.asarray(x), np.asarray(ctx_1024)
    row, head = np.arange(PART)[:, None], np.arange(HEADS)[None, :]
    inputs = {
        "xT": x.reshape(BATCHES, QUERIES, CHUNKS, PART).transpose(0, 3, 2, 1),
        "ctx": ctx,
        "ctxT": ctx.reshape(BATCHES, KEYS, CHUNKS, PART).transpose(0, 3, 2, 1),
        "wq": by_partition(L0_xattn_W_q),
        "wk": by_partition(L0_xattn_W_k),
        "wv": by_partition(L0_xattn_W_v),
        "wo": np.asarray(L0_xattn_W_o),
        "w1T": by_partition(np.asarray(L0_xattn_w1).T),
        "b1": np.asarray(L0_xattn_b1).reshape(CHUNKS, PART).T,
        "w2T": by_partition(np.asarray(L0_xattn_w2).T),
        "b2": np.asarray(L0_xattn_b2).reshape(CHUNKS, PART).T,
        "ident": np.eye(PART, dtype=np.float32),
        "pair_rows": (row // HEAD_DIM % 2 == head[:, :2]).astype(np.float32),
        "max_rows": (row == STACK + head).astype(np.float32),
    }
    inputs = {name + "_dram": np.ascontiguousarray(a) for name, a in inputs.items()}
    nc = bacc.Bacc("TRN2", target_bir_lowering=False, num_devices=1)
    args = [nc.dram_tensor(name, a.shape, mybir.dt.from_np(a.dtype), kind="ExternalInput").ap()
            for name, a in inputs.items()]
    outT = nc.dram_tensor("outT_dram", (BATCHES, PART, CHUNKS, QUERIES), mybir.dt.float32, kind="ExternalOutput").ap()
    cross_attention_ffn_attention(nc, *args, outT)
    result = run_bass_kernel_spmd(nc, [inputs], core_ids=[0]).results[0]["outT_dram"]
    return np.ascontiguousarray(result.transpose(0, 3, 2, 1)).reshape(BATCHES, QUERIES, DIM)
```
